# Optimizing a Trainium2 kernel written in Bass

```python
import numpy as np
import jax
import jax.numpy as jnp

def _softmax(x, axis=-1):
    return jax.nn.softmax(x, axis=axis)

def _gelu(x):
    return jax.nn.gelu(x, approximate=True)

def _silu(x):
    return jax.nn.silu(x)

def _sigmoid(x):
    return jax.nn.sigmoid(x)

def _layernorm(x, axis=-1, eps=1e-05):
    m = jnp.mean(x, axis=axis, keepdims=True)
    v = jnp.var(x, axis=axis, keepdims=True)
    return (x - m) / jnp.sqrt(v + eps)

def _scatter_add(tgt, idx, src, axis=0):
    return tgt.at[idx].add(src)

def _segment_sum(src, seg, n):
    return jax.ops.segment_sum(src, seg, n)
kernel_name = 'mk_flamingo_gated_d1_seqx_r8_58d7b4'

def setup_inputs(seed: int=0):
    np.random.seed(seed)
    _w = jnp.asarray

    def _rec_inputs():
        import jax
        import jax.numpy as jnp
        _rk = jax.random.key(seed)
        x = -0.0002928 + 1 * jax.random.normal(jax.random.fold_in(_rk, 1), (32, 128, 128), jnp.float32)
        _lenS = 128 - jax.random.randint(jax.random.fold_in(_rk, 7), (32,), 0, max(1, 128 // 4) + 1, jnp.int32)
        _lenS2 = 128 - jax.random.randint(jax.random.fold_in(_rk, 8), (32,), 0, max(1, 128 // 4) + 1, jnp.int32)
        _ctx_1024P = jax.random.normal(jax.random.fold_in(_rk, 11), (32, 16, 128), jnp.float32)
        _ctx_1024c = jax.random.dirichlet(jax.random.fold_in(_rk, 511), 0.3 * jnp.ones((16,), jnp.float32), (32, 128))
        _ctx_1024t = jnp.einsum('bsk,bkd->bsd', _ctx_1024c, _ctx_1024P)
        _ctx_1024t = _ctx_1024t * jax.lax.rsqrt(jnp.mean(jnp.square(_ctx_1024t)) + 1e-12) * 0.953939
        ctx_1024 = -1.39393e-06 + 0.999914 * (_ctx_1024t + 0.3 * jax.random.normal(jax.random.fold_in(_rk, 611), (32, 128, 128), jnp.float32))
        _g = jax.random.normal(jax.random.fold_in(_rk, 9001), (2, 1), jnp.float32)
        _g = jnp.sign(_g) * jnp.maximum(jnp.abs(_g), 1.0) + (_g == 0) * 1.0
        g_xattn = _g[0]
        g_ffn = _g[1]
        return (x, ctx_1024, g_xattn, g_ffn)
    x, ctx_1024, g_xattn, g_ffn = _rec_inputs()

    def _L0_xattn_setup():
        import jax, jax.numpy as jnp
        import numpy as np
        D_MODEL = 128
        NUM_HEADS = 16
        D_K = D_MODEL // NUM_HEADS
        SCALE = float(np.sqrt(D_K))
        key = jax.random.key(seed)
        ks = jax.random.split(key, 11)
        B, S = (2, 256)
        bound = float(np.sqrt(6.0 / (D_MODEL + D_MODEL)))

        def xavier(k):
            return jax.random.uniform(k, (D_MODEL, D_MODEL), jnp.float32, -bound, bound)
        return {'query': jax.random.normal(ks[0], (B, S, D_MODEL), jnp.float32), 'key': jax.random.normal(ks[1], (B, S, D_MODEL), jnp.float32), 'value': jax.random.normal(ks[2], (B, S, D_MODEL), jnp.float32), 'W_q': xavier(ks[3]), 'b_q': jnp.zeros((D_MODEL,), jnp.float32), 'W_k': xavier(ks[4]), 'b_k': jnp.zeros((D_MODEL,), jnp.float32), 'W_v': xavier(ks[5]), 'b_v': jnp.zeros((D_MODEL,), jnp.float32), 'W_o': xavier(ks[6]), 'b_o': jnp.zeros((D_MODEL,), jnp.float32)}
    _L0_xattn_all = _L0_xattn_setup()
    _L0_xattn_in = {k: v for k, v in _L0_xattn_all.items() if k in ('W_q', 'b_q', 'W_k', 'b_k', 'W_v', 'b_v', 'W_o', 'b_o')}
    del _L0_xattn_all

    def _L0_ffn_setup():
        import jax, jax.numpy as jnp
        import numpy as np
        NS, L, H = (8, 256, 128)
        M, E, K = (512, 8, 2)
        EPS = 1e-09
        key = jax.random.key(seed)
        ks = jax.random.split(key, 5)
        s = 0.02
        return {'x': jax.random.normal(ks[0], (NS, L, H), jnp.float32), 'Wr': jax.random.normal(ks[1], (H, E), jnp.float32) * s, 'br': jnp.zeros((E,), jnp.float32), 'W1': jax.random.normal(ks[2], (E, H, M), jnp.float32) * s, 'b1': jnp.zeros((E, M), jnp.float32), 'W2': jax.random.normal(ks[3], (E, M, H), jnp.float32) * s, 'b2': jnp.zeros((E, H), jnp.float32)}
    _L0_ffn_all = _L0_ffn_setup()
    _L0_ffn_in = {k: v for k, v in _L0_ffn_all.items() if k in ('Wr', 'br', 'W1', 'b1', 'W2', 'b2')}
    del _L0_ffn_all
    return {'x': x, 'ctx_1024': ctx_1024, 'g_xattn': g_xattn, 'g_ffn': g_ffn, 'L0_xattn_W_q': _L0_xattn_in['W_q'], 'L0_xattn_b_q': _L0_xattn_in['b_q'], 'L0_xattn_W_k': _L0_xattn_in['W_k'], 'L0_xattn_b_k': _L0_xattn_in['b_k'], 'L0_xattn_W_v': _L0_xattn_in['W_v'], 'L0_xattn_b_v': _L0_xattn_in['b_v'], 'L0_xattn_W_o': _L0_xattn_in['W_o'], 'L0_xattn_b_o': _L0_xattn_in['b_o'], 'L0_ffn_Wr': _L0_ffn_in['Wr'], 'L0_ffn_br': _L0_ffn_in['br'], 'L0_ffn_W1': _L0_ffn_in['W1'], 'L0_ffn_b1': _L0_ffn_in['b1'], 'L0_ffn_W2': _L0_ffn_in['W2'], 'L0_ffn_b2': _L0_ffn_in['b2']}

def reference(x, ctx_1024, g_xattn, g_ffn, L0_xattn_W_q, L0_xattn_b_q, L0_xattn_W_k, L0_xattn_b_k, L0_xattn_W_v, L0_xattn_b_v, L0_xattn_W_o, L0_xattn_b_o, L0_ffn_Wr, L0_ffn_br, L0_ffn_W1, L0_ffn_b1, L0_ffn_W2, L0_ffn_b2):
    import jax
    import jax.numpy as jnp

    def _L0_xattn_ref(query, key, value, W_q, b_q, W_k, b_k, W_v, b_v, W_o, b_o):
        import jax, jax.numpy as jnp
        import numpy as np
        D_MODEL = 128
        NUM_HEADS = 16
        D_K = D_MODEL // NUM_HEADS
        SCALE = float(np.sqrt(D_K))
        B, Sq, _ = query.shape
        Sk = key.shape[1]
        Q = query @ W_q.T + b_q
        K = key @ W_k.T + b_k
        V = value @ W_v.T + b_v
        Q = Q.reshape(B, Sq, NUM_HEADS, D_K).transpose(0, 2, 1, 3)
        K = K.reshape(B, Sk, NUM_HEADS, D_K).transpose(0, 2, 1, 3)
        V = V.reshape(B, Sk, NUM_HEADS, D_K).transpose(0, 2, 1, 3)
        scores = jnp.einsum('bhqd,bhkd->bhqk', Q, K) / SCALE
        attn = jax.nn.softmax(scores, axis=-1)
        attn = jnp.nan_to_num(attn, nan=0.0)
        context = jnp.einsum('bhqk,bhkd->bhqd', attn, V)
        context = context.transpose(0, 2, 1, 3).reshape(B, Sq, D_MODEL)
        output = context @ W_o.T + b_o
        return output

    def _L0_ffn_ref(x, Wr, br, W1, b1, W2, b2):
        import jax, jax.numpy as jnp
        import numpy as np
        NS, L, H = (8, 256, 128)
        M, E, K = (512, 8, 2)
        EPS = 1e-09
        ns, seq, h = x.shape
        flat = x.reshape(-1, h)
        logits = flat @ Wr + br
        probs = jax.nn.softmax(logits, axis=-1)
        vals, idx = jax.lax.top_k(probs, K)
        w = vals / (jnp.sum(vals, axis=-1, keepdims=True) + EPS)
        out_acc = jnp.zeros_like(flat)
        weight_acc = jnp.zeros((flat.shape[0],), flat.dtype)
        for e in range(E):
            we = jnp.sum(w * (idx == e), axis=-1)
            hmid = jax.nn.gelu(flat @ W1[e] + b1[e], approximate=False)
            y = hmid @ W2[e] + b2[e]
            out_acc = out_acc + we[:, None] * y
            weight_acc = weight_acc + we
        out = out_acc / (weight_acc[:, None] + EPS)
        return out.reshape(ns, seq, h)
    x = x + jnp.tanh(g_xattn[0]) * _L0_xattn_ref(_layernorm(x, axis=-1), ctx_1024, ctx_1024, L0_xattn_W_q, L0_xattn_b_q, L0_xattn_W_k, L0_xattn_b_k, L0_xattn_W_v, L0_xattn_b_v, L0_xattn_W_o, L0_xattn_b_o)
    x = x + jnp.tanh(g_ffn[0]) * _L0_ffn_ref(_layernorm(x, axis=-1), L0_ffn_Wr, L0_ffn_br, L0_ffn_W1, L0_ffn_b1, L0_ffn_W2, L0_ffn_b2)
    return x

_drawn_inputs = setup_inputs


def setup_inputs(seed=0):
    import zlib

    import numpy as np

    out = dict(_drawn_inputs(seed))
    spreads = {'L0_xattn_b_q': (0.0, 0.43),
     'L0_xattn_b_k': (0.0, 0.8),
     'L0_xattn_b_v': (0.0, 0.1),
     'L0_xattn_b_o': (0.0, 0.1),
     'L0_ffn_br': (0.0, 0.1),
     'L0_ffn_b1': (0.0, 0.564),
     'L0_ffn_b2': (0.0, 0.1)}
    factors = {}
    for name, (base, spread) in spreads.items():
        noise = np.random.default_rng([zlib.crc32(name.encode()), seed]).standard_normal(out[name].shape)
        drawn = base * np.exp(spread * noise) if base else spread * noise
        out[name] = jnp.asarray(drawn.astype(out[name].dtype))
    for name, factor in factors.items():
        out[name] = (out[name] * factor).astype(out[name].dtype)
    return out
```

```python
from contextlib import ExitStack

import numpy as np

import concourse.bass as bass
from concourse import mybir

ALU = mybir.AluOpType
ACT = mybir.ActivationFunctionType
AX_X = mybir.AxisListType.X
F32 = mybir.dt.float32
F16 = mybir.dt.float16
BF16 = mybir.dt.bfloat16
I32 = mybir.dt.int32
U32 = mybir.dt.uint32

P = 128
NB = 32
D = 128
NH, DK = 16, 8
NJ, NS = 4, 4
GB = 4
NG = NB // GB
GT = GB * P
UPG = GB * NS
E, M, TOPK = 8, 512, 2
MC = M // P
NTOK = NB * P
TR = 256
NT = (TOPK * NTOK + E * (TR - 1)) // TR
RS = NTOK + TR
ROWS = E * RS + TR
PW = D + 2
MAXT = NTOK // TR
LN_EPS, MOE_EPS = 1e-5, 1e-9
W1_SCALE = 64.0
NOWHERE = float(4 * NTOK)
PING = 3

C_IOTA, C_BASE, C_TILE, C_STEP, C_ID = 0, E, 2 * E, 2 * E + NT, 2 * E + NT + MAXT
C_END = C_ID + NB * TOPK


def wait(eng, sem, value):
    if isinstance(value, int) and value <= 0:
        return
    eng.wait_ge(sem, value)


class Chain:

    def __init__(self, eng, sem, per, n):
        self.eng, self.sem, self.per, self.n, self.count = eng, sem, per, n, 0

    def step(self, ins):
        self.count += 1
        assert self.count <= self.per
        ins.then_inc(self.sem, 1)

    def settle(self):
        self.eng.wait_ge(self.sem, self.n * self.per + self.count)

    def link(self, ins):
        self.step(ins)
        self.settle()


def moe_attention(nc, x, ctx_in, gates, wq, bq, wk, bk, wv, bv, wo, bo, wr, br, w1, b1, w2, b2, ident_in, tri_in, consts_in, out):
    bounce = {t: nc.dram_tensor(f"bounce_{t}", (NJ, 4, DK, NS, GT), F16, kind="Internal").ap() for t in "qk"}
    rows_dram = nc.dram_tensor("rows_dram", (ROWS, PW), F32, kind="Internal").ap()
    y_dram = nc.dram_tensor("y_dram", (TOPK * NTOK, D), F32, kind="Internal").ap()

    with ExitStack() as stack:
        def sb(name, shape, dt=F32):
            return stack.enter_context(nc.sbuf_tensor(name, shape, dt))

        def psum(name, shape):
            return stack.enter_context(nc.psum_tensor(name, shape, F32))

        def sem(name):
            return stack.enter_context(nc.semaphore(name))

        ident = sb("ident", [P, P])
        neg_ident = sb("neg_ident", [P, P], BF16)
        tri32 = sb("tri32", [P, P])
        tri = sb("tri", [P, P], BF16)
        ones = sb("ones", [P, P], BF16)
        consts = sb("consts", [P, C_END])
        gate_in = sb("gate_in", [P, 2])
        gate = sb("gate", [P, 2])
        neg_half = sb("neg_half", [P, NB])
        wqT, wkT, wvT, woT = (sb(n, [P, D]) for n in ("wqT", "wkT", "wvT", "woT"))
        bq_c, bk_c = sb("bq_c", [P, 1]), sb("bk_c", [P, 1])
        bv_b, bo_b, gbo = sb("bv_b", [P, D]), sb("bo_b", [P, D]), sb("gbo", [P, D])
        wr_sb, br_b = sb("wr_sb", [P, E]), sb("br_b", [P, E])
        w1_stage = sb("w1_stage", [P, M])
        w1_hi, w1_lo = sb("w1_hi", [P, E, M], F16), sb("w1_lo", [P, E, M], F16)
        b1_c = sb("b1_c", [P, E * MC])
        w2_sb = sb("w2_sb", [P, E * MC, D])
        b2_b = sb("b2_b", [P, E, D])
        x_all = sb("x_all", [P, NB, D])
        c_in = sb("c_in", [P, GB, D])
        xn = sb("xn", [P, GB, D])
        st1, mv1, rs1, nb1 = sb("st1", [P, NB, 6]), sb("mv1", [P, NB, 2]), sb("rs1", [P, NB]), sb("nb1", [P, NB])
        st2, mv2, rs2, nb2 = sb("st2", [P, GB, 6]), sb("mv2", [P, 2, GB, 2]), sb("rs2", [P, GB]), sb("nb2", [P, GB])
        xnT, cT = sb("xnT", [P, GT]), sb("cT", [P, GT])
        parts = {t: sb(f"parts_{t}", [P, 2, GT], F16) for t in "qk"}
        plain = {t: sb(f"plain_{t}", [P, 2, NS, GT], F16) for t in "qk"}
        diag = {t: sb(f"diag_{t}", [P, 2, NJ, NS, GT], F16) for t in "qk"}
        v_aug = sb("v_aug", [P, GB, NH, 32])
        maxes = sb("maxes", [P, UPG, NJ], BF16)
        probs = sb("probs", [P, 4, NJ, P])
        o_sb = sb("o_sb", [P, NS * P])
        rl = sb("rl", [P, NS, NJ])
        a_sb, aT = sb("a_sb", [P, D]), sb("aT", [P, P])
        pay = sb("pay", [P, 2, GB, TOPK, PW])
        x2T = sb("x2T", [P, GT])
        lg, t8, dz, ez = (sb(n, [P, GB, E]) for n in ("lg", "t8", "dz", "ez"))
        ti, tif = sb("ti", [P, GB, E], U32), sb("tif", [P, GB, TOPK])
        mk, mboth = sb("mk", [P, GB, TOPK, E]), sb("mboth", [P, GB, E], BF16)
        mcarry, msum = sb("mcarry", [P, E], BF16), sb("msum", [P, E])
        z1, z2, z3, z4, z5, z6, z7, z8 = (sb(f"z{i}", [P, GB]) for i in range(8))
        pk, wk2 = sb("pk", [P, GB, TOPK]), sb("wk2", [P, GB, TOPK])
        rank_b, sel, slot_f = sb("rank_b", [P, GB, E]), sb("sel", [P, GB, TOPK, E]), sb("slot_f", [P, GB, TOPK])
        slot_i = sb("slot_i", [P, 2, GB * TOPK], I32)
        cnt, fill_f, fill_i = sb("cnt", [P, E]), sb("fill_f", [P, E]), sb("fill_i", [P, E], I32)
        over, ntile, ntile_end = sb("over", [P, E, MAXT]), sb("ntile", [P, E]), sb("ntile_end", [P, E])
        past, pastn = sb("past", [P, NT, E]), sb("pastn", [P, NT, E])
        te, tprev, ta, tb, tr = (sb(n, [P, NT]) for n in ("te", "tprev", "ta", "tb", "tr"))
        tile_row, tile_e = sb("tile_row", [P, NT], I32), sb("tile_e", [P, NT], I32)
        pad = sb("pad", [P, 2, PW])
        ones8 = sb("ones8", [P, E])
        xt = sb("xt", [P, PING, 2, PW])
        xh, xl = sb("xh", [P, PING, TR], F16), sb("xl", [P, PING, TR], F16)
        room = diag["k"][:, :, :, :, :].rearrange("p a j s t -> p (a j s t)").bitcast(F32)
        n_h, n_y, n_r = PING * MC * TR, 2 * TOPK * GB * D, 2 * GB * D
        hT = room[:, 0:n_h].rearrange("p (r c t) -> p r c t", r=PING, c=MC)
        yb, ys = sb("yb", [P, PING, 2, D]), sb("ys", [P, PING, 2, D])
        dest = sb("dest", [P, PING, 2], I32)
        meta = sb("meta", [P, PING, 2, 2])
        y_in = room[:, n_h:n_h + n_y].rearrange("p (r k b d) -> p r k b d", r=2, k=TOPK, b=GB)
        res = room[:, n_h + n_y:n_h + n_y + n_r].rearrange("p (r b d) -> p r b d", r=2, b=GB)

        s_bank = [psum(f"s_bank{i}", [P, 512]) for i in range(2)]
        t_bank = [psum(f"t_bank{i}", [P, 512]) for i in range(2)]
        o_bank = [psum(f"o_bank{i}", [P, 512]) for i in range(2)]
        prep = psum("prep", [P, 512])
        tail = psum("tail", [P, 512])
        h_bank = [[s_bank[0], s_bank[1]], [t_bank[0], t_bank[1]], [o_bank[0], o_bank[1]]]
        xT_bank, y_bank = prep, tail

        x_first, x_rest, w_in, w_in2 = sem("x_first"), sem("x_rest"), sem("w_in"), sem("w_in2")
        c_ready, w1_ready = sem("c_ready"), sem("w1_ready")
        bounced = {t: sem(f"bounced_{t}") for t in "qk"}
        spread = {t: sem(f"spread_{t}") for t in "qk"}
        scattered, filled = [sem(f"scattered{i}") for i in range(2)], sem("filled")
        setup, gates_done, zeroed = sem("setup"), sem("gates_done"), [sem(f"zeroed{i}") for i in range(2)]
        tri_done, pad_done, v_zeroed = sem("tri_done"), sem("pad_done"), sem("v_zeroed")
        gbo_done, setup_pool = sem("gbo_done"), sem("setup_pool")
        prep_full, v_done, xc_done = sem("prep_full"), sem("v_done"), sem("xc_done")
        tail_full, tail_free = sem("tail_full"), sem("tail_free")
        scored, maxed, scoredT, exped, pv_done, o_out = (sem(n) for n in ("scored", "maxed", "scoredT", "exped", "pv_done", "o_out"))
        ln1_stats, ln1_rs, ln1_done, x_plus = (sem(n) for n in ("ln1_stats", "ln1_rs", "ln1_done", "x_plus"))
        ln2_stats, ln2_rs, ln2_done = (sem(n) for n in ("ln2_stats", "ln2_rs", "ln2_done"))
        hi_done, lo_done = sem("hi_done"), sem("lo_done")
        norm_c, x2_done, route_c, ez_done, ids_done = (sem(n) for n in ("norm_c", "x2_done", "route_c", "ez_done", "ids_done"))
        w1hi_done, w1lo_done = sem("w1hi_done"), sem("w1lo_done")
        cnt_full, table_c = sem("cnt_full"), sem("table_c")
        taken = sem("taken")
        x_tile = [sem(f"x_tile{i}") for i in range(PING)]
        y_tile = [sem(f"y_tile{i}") for i in range(PING)]
        xT_full, xh_done, xl_done = sem("xT_full"), sem("xh_done"), sem("xl_done")
        h_full, h_done, y_full, yb_done, ys_done, dest_done = (sem(n) for n in ("h_full", "h_done", "y_full", "yb_done", "ys_done", "dest_done"))
        y_ready = [sem(f"y_ready{i}") for i in range(2)]
        sum_c = sem("sum_c")
        out_done = [sem(f"out_done{i}") for i in range(2)]
        RSTEPS, ROUTE, R_DIFF, R_MASK, TABLE = 4, 22, 3, 6, 15

        def prep_use(g, what):
            return 7 + 8 * g + PREP.index(what)

        PREP = ("V3", "xT", "cT", "Q", "V0", "K", "V1", "V2")

        def prep_done(g, what):
            if what[0] == "V":
                return v_done, 4 * g + 4 + ("V3", "V0", "V1", "V2").index(what)
            if what in ("xT", "cT"):
                return xc_done, 2 * g + 3 + (what == "cT")
            return lo_done, 2 * g + 3 + (what == "K")

        order = ["OT3", "aT3", "y3", "OT0", "aT0", "y0", "x2T", "OT1", "logits", "aT1", "y1", "OT2", "rank", "aT2", "y2"]
        first = [w for w in order if w[:-1] in ("OT", "aT", "y") and w[-1] != "3"]

        def tail_use(g, what):
            if isinstance(g, int) and g == 0:
                return first.index(what)
            if isinstance(g, int) and g == NG:
                return 15 * NG - 6 + ["OT3", "aT3", "y3", "x2T", "logits", "rank"].index(what)
            return 15 * g - 6 + order.index(what)

        def bodies(eng, body):
            body(0, 0, True, False, 0)
            with eng.Fori(0, (NG - 2) // 2) as n:
                body(n * 2 + 1, 1, False, False, n)
                body(n * 2 + 2, 0, False, False, n)
            body(NG - 1, 1, False, True, NG // 2 - 1)

        waited = {e: sem(f"waited_{n}") for n, e in (("sp", nc.sync.engine), ("dve", nc.vector.engine), ("pool", nc.gpsimd.engine))}

        def apart(eng):
            eng.sem_inc(waited[eng.engine], 1)

        block = stack.enter_context(nc.Block())

        @block.sync
        def _(sp):
            xv = x.rearrange("b p d -> p b d")
            cv = ctx_in.rearrange("b p d -> p b d")
            sp.dma_start(x_all[:, 0:GB, :], xv[:, 0:GB, :]).then_inc(x_first, 16)
            sp.dma_start(c_in[:, :, :], cv[:, 0:GB, :]).then_inc(c_ready, 16)
            small = [(gate_in[:, :], gates.partition_broadcast(P)), (ident[:, :], ident_in), (wqT[:, :], wq), (wkT[:, :], wk), (wvT[:, :], wv),
                     (bq_c[:, :], bq), (bk_c[:, :], bk), (bv_b[:, :], bv.partition_broadcast(P)), (bo_b[:, :], bo.partition_broadcast(P))]
            for dst, src in small:
                sp.dma_start(dst, src).then_inc(w_in, 16)
            sp.dma_start(x_all[:, GB:NB, :], xv[:, GB:NB, :]).then_inc(x_rest, 16)
            late = [(woT[:, :], wo), (wr_sb[:, :], wr), (br_b[:, :], br.partition_broadcast(P)), (tri32[:, :], tri_in),
                    (consts[:, :], consts_in),
                    (b1_c[:, :], b1), (b2_b[:, :, :], b2.partition_broadcast(P)), (w2_sb[:, :, :], w2)]
            for dst, src in late:
                sp.dma_start(dst, src).then_inc(w_in2, 16)

            def spread_part(G, par, t, n):
                wait(sp, lo_done, 2 * G + n + 1)
                apart(sp)
                wait(sp, spread[t], 16 * 5 * G)
                for r in range(4):
                    part = r >> 1 if t == "q" else r & 1
                    sp.dma_start(bounce[t][:, r].rearrange("j i s t -> j (i s) t"), parts[t][:, part, :]).then_inc(bounced[t], 16)
                sp.wait_ge(bounced[t], 16 * 4 * (G + 1))
                apart(sp)
                wait(sp, scoredT, UPG * (G - 1))
                sp.wait_ge(zeroed[par], 2)
                sp.dma_start(plain[t][:, par], bounce[t].rearrange("j r i s t -> (j r i) s t")).then_inc(spread[t], 16)
                for j in range(NJ):
                    sp.dma_start(diag[t][32 * j:32 * j + 32, par, j], bounce[t][j].rearrange("r i s t -> (r i) s t")).then_inc(spread[t], 16)

            def body(g, par, is_first, is_last, pairs):
                wait(sp, w1lo_done, g)
                sp.dma_start(w1_stage[:, :], w1[g]).then_inc(w1_ready, 16)
                if is_last:
                    return
                sp.wait_ge(prep_full, prep_use(g - 1, "cT") + 1)
                apart(sp)
                sp.dma_start(c_in[:, :, :], cv[:, bass.ds(g * GB + GB, GB), :]).then_inc(c_ready, 16)
                spread_part(g + 1, 1 - par, "q", 0)
                spread_part(g + 1, 1 - par, "k", 1)

            spread_part(0, 0, "q", 0)
            spread_part(0, 0, "k", 1)
            bodies(sp, body)

            for i in range(2):
                sp.wait_ge(scattered[i], 16 * GB * TOPK * NG // 2)
            sp.wait_ge(table_c, TABLE)
            for e in range(E):
                at = sp.value_load(fill_i[0:1, e:e + 1], min_val=e * RS, max_val=e * RS + NTOK)
                sp.dma_start(rows_dram[bass.ds(at, TR), :].rearrange("(p h) c -> p h c", h=2), pad[:, :, :]).then_inc(filled, 16)
            sp.dma_start(rows_dram[E * RS:ROWS, :].rearrange("(p h) c -> p h c", h=2), pad[:, :, :]).then_inc(filled, 16)
            sp.wait_ge(filled, 16 * (E + 1))

            def load_tile(i, r):
                wait(sp, taken, i - PING + 1)
                apart(sp)
                at = sp.value_load(tile_row[0:1, i:i + 1] if isinstance(i, int) else tile_row[0:1, bass.ds(i, 1)], min_val=0, max_val=E * RS)
                sp.dma_start(xt[:, r], rows_dram[bass.ds(at, TR), :].rearrange("(p h) c -> p h c", h=2)).then_inc(x_tile[r], 16)

            for r in range(PING):
                load_tile(r, r)
            with sp.Fori(1, NT // PING) as n:
                for r in range(PING):
                    load_tile(n * PING + r, r)

            for r in range(PING):
                sp.wait_ge(y_tile[r], 32 * (NT // PING))
            yv = y_dram.rearrange("(k b p) d -> k p b d", k=TOPK, p=P)
            ov = out.rearrange("b p d -> p b d")

            for g in range(NG):
                if g >= 2:
                    sp.wait_ge(sum_c, 2 * g - 2)
                for k in range(TOPK):
                    sp.dma_start(y_in[:, g % 2, k], yv[k][:, g * GB:(g + 1) * GB, :]).then_inc(y_ready[g % 2], 16)
                if g >= 1:
                    sp.wait_ge(sum_c, 2 * g)
                    sp.dma_start(ov[:, (g - 1) * GB:g * GB, :], res[:, (g - 1) % 2]).then_inc(out_done[(g - 1) % 2], 16)
            sp.wait_ge(sum_c, 2 * NG)
            sp.dma_start(ov[:, (NG - 1) * GB:, :], res[:, (NG - 1) % 2]).then_inc(out_done[(NG - 1) % 2], 16)
            for r in range(2):
                sp.wait_ge(out_done[r], 16 * (NG // 2))

        @block.tensor
        def _(pe):
            def prep_begin(g, what):
                if what == "V3":
                    wait(pe, *prep_done(g - 1, "V2"))
                elif not (what == "xT" and isinstance(g, int) and g < 0):
                    wait(pe, *prep_done(g, PREP[PREP.index(what) - 1]))

            def tail_begin(g, what):
                wait(pe, tail_free, tail_use(g, what))

            def scores(g, par, u):
                if u == 0:
                    for t in "qk":
                        pe.wait_ge(spread[t], 16 * 5 * (g + 1))
                wait(pe, maxed, UPG * g + u - 1)
                b, s = u // NS, u % NS
                toks = slice(b * P, (b + 1) * P)
                nc.tensor.matmul(s_bank[u % 2][:, :], plain["q"][:, par, s, toks], diag["k"][:, par, :, s, toks],
                                 start=True, stop=True).then_inc(scored, 1)

            def scores_T(g, par, u):
                b, s = u // NS, u % NS
                toks = slice(b * P, (b + 1) * P)
                bank = t_bank[u % 2]
                wait(pe, exped, UPG * g + u - 1)
                nc.tensor.matmul(bank[:, :], plain["k"][:, par, s, toks], diag["q"][:, par, :, s, toks], start=True, stop=False,
                                 skip_group_check=True)
                pe.wait_ge(maxed, UPG * g + u + 1)
                for j in range(NJ):
                    last = nc.tensor.matmul(bank[:, j * P:(j + 1) * P], maxes[:, u, j:j + 1].broadcast_to([P, P]), neg_ident[:, :],
                                            start=False, stop=True, skip_group_check=True)
                last.then_inc(scoredT, 1)

            def values(g, u):
                if u < 0:
                    g, u = g - 1, UPG - 1
                b, s = u // NS, u % NS
                pe.wait_ge(exped, UPG * g + u + 1)
                if s == 0:
                    what = f"V{b}"
                    wait(pe, *prep_done(g if b == 3 else g - 1, what))
                    wait(pe, o_out, GB * g + b - 1)
                for j in range(NJ):
                    last = nc.tensor.matmul(o_bank[b % 2][32 * j:32 * j + 32, s * P:(s + 1) * P], v_aug[:, b, NJ * j + s, :],
                                            probs[:, u % 4, j, :], start=True, stop=True)
                last.then_inc(pv_done, 1)

            def project_v(g, b):
                prep_begin(g, f"V{b}")
                nc.tensor.matmul(prep[:, 0:D], cT[:, b * P:(b + 1) * P], wvT[:, :], start=True, stop=True).then_inc(prep_full, 1)

            def transpose4(bank, src):
                for b in range(GB):
                    last = nc.tensor.transpose(bank[:, b * P:(b + 1) * P], src(b), ident[:, :])
                return last

            def prep_x(g):
                prep_begin(g, "xT")
                pe.wait_ge(ln1_done, g + 2)
                transpose4(prep, lambda b: xn[:, b, :]).then_inc(prep_full, 1)

            def prep_c(g):
                prep_begin(g, "cT")
                pe.wait_ge(c_ready, 16 * (g + 2))
                transpose4(prep, lambda b: c_in[:, b, :]).then_inc(prep_full, 1)

            def prep_q(g):
                prep_begin(g, "Q")
                nc.tensor.matmul(prep[:, :], wqT[:, :], xnT[:, :], start=True, stop=True).then_inc(prep_full, 1)

            def prep_k(g):
                prep_begin(g, "K")
                nc.tensor.matmul(prep[:, :], wkT[:, :], cT[:, :], start=True, stop=True).then_inc(prep_full, 1)

            def o_T(g, b):
                tail_begin(g, f"OT{b}")
                pe.wait_ge(o_out, GB * g + (b + 1 if b < 3 else 0))
                transpose4(tail, lambda s: o_sb[:, s * P:(s + 1) * P]).then_inc(tail_full, 1)

            def a_T(g, b):
                tail_begin(g, f"aT{b}")
                nc.tensor.transpose(tail[:, 0:P], a_sb[:, :], ident[:, :]).then_inc(tail_full, 1)

            def y_out(g, b):
                tail_begin(g, f"y{b}")
                nc.tensor.matmul(tail[:, 0:D], aT[:, :], woT[:, :], start=True, stop=True).then_inc(tail_full, 1)

            def x2_T(g, par):
                tail_begin(g, "x2T")
                pe.wait_ge(ln2_done, g)
                transpose4(tail, lambda b: pay[:, par, b, 0, 0:D]).then_inc(tail_full, 1)

            def logits(g):
                tail_begin(g, "logits")
                for b in range(GB):
                    last = nc.tensor.matmul(tail[:, b * E:(b + 1) * E], x2T[:, b * P:(b + 1) * P], wr_sb[:, :], start=True, stop=True)
                last.then_inc(tail_full, 1)

            def rank(g):
                tail_begin(g, "rank")
                pe.wait_ge(route_c, ROUTE * (g - 1) + R_MASK)
                out4 = tail[:, 0:GB * E].rearrange("p (b e) -> p b e", b=GB)
                nc.tensor.matmul(out4, tri[:, :], mboth[:, :, :], start=True, stop=False, skip_group_check=True)
                for k in range(1, GB):
                    nc.tensor.matmul(out4[:, k:GB, :], ones[:, :], mboth[:, 0:GB - k, :], start=False, stop=False, skip_group_check=True)
                nc.tensor.matmul(out4, ones[:, :], mcarry[:, :].unsqueeze(1).broadcast_to([P, GB, E]), start=False, stop=True,
                                 skip_group_check=True).then_inc(tail_full, 1)

            def body(g, par, is_first, is_last, pairs):
                for u in range(UPG):
                    if u < UPG - 2:
                        scores(g, par, u + 2)
                    elif not is_last:
                        scores(g + 1, 1 - par, u + 2 - UPG)
                    scores_T(g, par, u)
                    if not (is_first and u == 0):
                        values(g, u - 1)
                    if u == 1:
                        project_v(g, 3)
                        if not is_first:
                            o_T(g, 3)
                    if u == 2:
                        if not is_last:
                            prep_x(g)
                        if not is_first:
                            a_T(g, 3)
                    if u == 3:
                        if not is_last:
                            prep_c(g)
                        if not is_first:
                            y_out(g, 3)
                    if u == 4 and not is_last:
                        prep_q(g)
                    if u in (5, 9, 13):
                        if not is_last:
                            project_v(g, (u - 5) // 4)
                        o_T(g, (u - 5) // 4)
                    if u == 6 and not is_last:
                        prep_k(g)
                    if u in (6, 10, 14):
                        a_T(g, (u - 6) // 4)
                    if u in (7, 11, 15):
                        y_out(g, (u - 7) // 4)
                    if not is_first:
                        if u == 8:
                            x2_T(g, 1 - par)
                        if u == 9:
                            logits(g)
                        if u == 13:
                            rank(g)

            pe.wait_ge(w_in, 16 * 9)
            pe.wait_ge(setup, 2)
            prep_x(-1)
            prep_c(-1)
            prep_q(-1)
            project_v(-1, 0)
            prep_k(-1)
            project_v(-1, 1)
            project_v(-1, 2)
            scores(0, 0, 0)
            scores(0, 0, 1)
            pe.wait_ge(w_in2, 16 * 8)
            bodies(pe, body)
            values(NG, -1)
            o_T(NG, 3)
            a_T(NG, 3)
            y_out(NG, 3)
            x2_T(NG, 1)
            logits(NG)
            rank(NG)
            wait(pe, tail_free, 15 * NG)
            pe.wait_ge(route_c, ROUTE * NG)
            nc.tensor.matmul(tail[:, 0:E], ones[:, :], mcarry[:, :], start=True, stop=True).then_inc(cnt_full, 1)
            pe.wait_ge(table_c, TABLE)

            def x_T(i, r, turn):
                pe.wait_ge(x_tile[r], 16 * (turn + 1))
                wait(pe, xl_done, i)
                for h in range(2):
                    last = nc.tensor.transpose(xT_bank[:, h * P:(h + 1) * P], xt[:, r, h, 0:D], ident[:, :])
                last.then_inc(xT_full, 1)

            def up(i, r):
                e = pe.value_load(tile_e[0:1, i:i + 1] if isinstance(i, int) else tile_e[0:1, bass.ds(i, 1)], min_val=0, max_val=E - 1)
                pe.wait_ge(xl_done, i + 1)
                wait(pe, h_done, MC * (i - 2))
                for c in range(MC):
                    o = h_bank[r][c // 2][:, (c % 2) * TR:(c % 2) * TR + TR]
                    cols = slice(c * P, (c + 1) * P)
                    nc.tensor.matmul(o, w1_hi[:, e, cols], xh[:, r, :], start=True, stop=False)
                    nc.tensor.matmul(o, w1_hi[:, e, cols], xl[:, r, :], start=False, stop=False)
                    nc.tensor.matmul(o, w1_lo[:, e, cols], xh[:, r, :], start=False, stop=True).then_inc(h_full, 1)

            def down(i, r):
                e = pe.value_load(tile_e[0:1, i:i + 1] if isinstance(i, int) else tile_e[0:1, bass.ds(i, 1)], min_val=0, max_val=E - 1)
                wait(pe, yb_done, i)
                for h in range(2):
                    for c in range(MC):
                        if h == 0:
                            pe.wait_ge(h_done, MC * i + c + 1)
                        last = nc.tensor.matmul(y_bank[:, h * D:(h + 1) * D], hT[:, r, c, h * P:(h + 1) * P], w2_sb[:, e * MC + c, :],
                                                start=(c == 0), stop=(c == MC - 1), skip_group_check=True)
                last.then_inc(y_full, 1)

            x_T(0, 0, 0)
            x_T(1, 1, 0)
            up(0, 0)

            def tiles(n, is_last):
                for r in range(PING):
                    i = n * PING + r
                    if not (is_last and r >= PING - 2):
                        x_T(i + 2, (r + 2) % PING, n if r == 0 else n + 1)
                    if not (is_last and r >= PING - 1):
                        up(i + 1, (r + 1) % PING)
                    down(i, r)

            tiles(0, False)
            with pe.Fori(1, NT // PING - 1) as n:
                tiles(n, False)
            tiles(NT // PING - 1, True)

        @block.scalar
        def _(act):
            def col(t, i):
                return t[:, i:i + 1] if isinstance(i, int) else t[:, bass.ds(i, 1)]

            copy = lambda out_, in_: nc.scalar.activation(out_, in_, ACT.Copy)

            def exp(g, u):
                act.wait_ge(scoredT, UPG * g + u + 1)
                wait(act, pv_done, UPG * g + u - 3)
                nc.scalar.activation(probs[:, u % 4].rearrange("p j q -> p (j q)"), t_bank[u % 2][:, :], ACT.Exp,
                                     scale=DK ** -0.5).then_inc(exped, 1)

            def prep_copy(g, what, dst):
                act.wait_ge(prep_full, prep_use(g, what) + 1)
                copy(dst, prep[:, :]).then_inc(xc_done, 1)

            def split_hi(g, t, n):
                act.wait_ge(prep_full, prep_use(g, t.upper()) + 1)
                wait(act, bounced[t], 16 * 4 * (g + 1))
                nc.scalar.activation(parts[t][:, 0, :], prep[:, :], ACT.Identity, bias=(bq_c if t == "q" else bk_c)[:, 0:1]).then_inc(hi_done, 1)

            def ln1(g):
                act.wait_ge(ln1_rs, RSTEPS if isinstance(g, int) and g < 0 else 2 * RSTEPS)
                wait(act, prep_full, prep_use(g - 1, "xT") + 1)
                for b in range(GB):
                    last = nc.scalar.activation(xn[:, b, :], x_all[:, g * GB + GB + b, :], ACT.Identity, bias=col(nb1, g * GB + GB + b), scale=col(rs1, g * GB + GB + b))
                last.then_inc(ln1_done, 1)

            def o_copy(g, b):
                done = NS * (GB * g + (b + 1 if b < 3 else 0))
                act.wait_ge(pv_done, done)
                if b < 3 and isinstance(g, int) and g == 0 and b == 0:
                    pass
                else:
                    act.wait_ge(tail_full, (tail_use(g - 1, "OT2") if b == 3 else tail_use(g, "OT3" if b == 0 else f"OT{b - 1}")) + 1)
                copy(o_sb[:, :], o_bank[b % 2][:, :]).then_inc(o_out, 1)

            def a_copy(g, b):
                act.wait_ge(tail_full, tail_use(g, f"aT{b}") + 1)
                copy(aT[:, :], tail[:, 0:P]).then_inc(tail_free, 1)

            def ln2(g, par):
                act.wait_ge(ln2_rs, RSTEPS * g)
                for b in range(GB):
                    last = nc.scalar.activation(pay[:, par, b, :, 0:D], x_all[:, g * GB - GB + b, :].unsqueeze(1).broadcast_to([P, TOPK, D]), ACT.Identity,
                                                bias=nb2[:, b:b + 1], scale=rs2[:, b:b + 1])
                last.then_inc(ln2_done, 1)

            def x2_copy(g):
                act.wait_ge(tail_full, tail_use(g, "x2T") + 1)
                copy(x2T[:, :], tail[:, :]).then_inc(tail_free, 1)

            def route_exp(g):
                act.wait_ge(route_c, ROUTE * (g - 1) + R_DIFF)
                nc.scalar.activation(ez[:, :, :], dz[:, :, :], ACT.Exp).then_inc(ez_done, 1)

            def w1_split(g):
                act.wait_ge(w1_ready, 16 * (g + 1))
                nc.scalar.activation(w1_hi[:, g, :], w1_stage[:, :], ACT.Copy, scale=W1_SCALE).then_inc(w1hi_done, 1)

            def body(g, par, is_first, is_last, pairs):
                for u in range(UPG):
                    exp(g, u)
                    if u == 0 and not is_first:
                        o_copy(g, 3)
                    if u == 1 and not is_last:
                        ln1(g)
                    if u == 2:
                        if not is_last:
                            prep_copy(g, "xT", xnT[:, :])
                        if not is_first:
                            a_copy(g, 3)
                    if u == 3 and not is_last:
                        prep_copy(g, "cT", cT[:, :])
                    if u == 4 and not is_last:
                        split_hi(g, "q", 0)
                    if u in (4, 8, 12):
                        o_copy(g, u // 4 - 1)
                    if u == 6 and not is_last:
                        split_hi(g, "k", 1)
                    if u in (6, 10, 14):
                        a_copy(g, (u - 6) // 4)
                    if u == 7 and not is_first:
                        ln2(g, 1 - par)
                    if u == 8 and not is_first:
                        x2_copy(g)
                    if u == 9:
                        w1_split(g)
                    if u == 11 and not is_first:
                        route_exp(g)

            act.wait_ge(w_in, 16 * 9)
            nc.scalar.activation(gate[:, :], gate_in[:, :], ACT.Tanh).then_inc(gates_done, 1)
            ln1(-1)
            prep_copy(-1, "xT", xnT[:, :])
            prep_copy(-1, "cT", cT[:, :])
            split_hi(-1, "q", 0)
            split_hi(-1, "k", 1)
            bodies(act, body)
            o_copy(NG, 3)
            a_copy(NG, 3)
            ln2(NG, 1)
            x2_copy(NG)
            route_exp(NG)
            act.wait_ge(table_c, TABLE)

            def x_hi(i, r):
                act.wait_ge(xT_full, i + 1)
                copy(xh[:, r, :], xT_bank[:, 0:TR]).then_inc(xh_done, 1)

            def gelu(i, r):
                e = act.value_load(tile_e[0:1, i:i + 1] if isinstance(i, int) else tile_e[0:1, bass.ds(i, 1)], min_val=0, max_val=E - 1)
                wait(act, y_full, i - 2)
                for c in range(MC):
                    act.wait_ge(h_full, MC * i + c + 1 if c % 2 else MC * i + c + 2)
                    nc.scalar.activation(hT[:, r, c, :], h_bank[r][c // 2][:, (c % 2) * TR:(c % 2) * TR + TR], ACT.Gelu,
                                         bias=b1_c[:, bass.ds(e * MC + c, 1)], scale=1.0 / W1_SCALE).then_inc(h_done, 1)

            x_hi(0, 0)
            x_hi(1, 1)

            def tiles(n, is_last):
                for r in range(PING):
                    i = n * PING + r
                    gelu(i, r)
                    if not (is_last and r >= PING - 2):
                        x_hi(i + 2, (r + 2) % PING)

            tiles(0, False)
            with act.Fori(1, NT // PING - 1) as n:
                tiles(n, False)
            tiles(NT // PING - 1, True)

        @block.vector
        def _(dve):
            vec = nc.vector

            def maxima(g, u):
                dve.wait_ge(scored, UPG * g + u + 1)
                vec.reduce_max(maxes[:, u, :], s_bank[u % 2][:, :].rearrange("p (j k) -> p j k", j=NJ), AX_X).then_inc(maxed, 1)

            def v_out(g, b):
                dve.wait_ge(prep_full, prep_use(g, f"V{b}") + 1)
                vec.tensor_tensor(v_aug[:, b, :, 0:DK], prep[:, 0:D].rearrange("p (h d) -> p h d", h=NH),
                                  bv_b[:, :].rearrange("p (h d) -> p h d", h=NH), ALU.add).then_inc(v_done, 1)

            def split_lo(g, t, n):
                dve.wait_ge(hi_done, 2 * g + 2 + n + 1)
                wait(dve, bounced[t], 16 * 4 * (g + 1))
                vec.scalar_tensor_tensor(parts[t][:, 1, :], prep[:, :], (bq_c if t == "q" else bk_c)[:, 0:1], parts[t][:, 0, :],
                                         ALU.add, ALU.subtract).then_inc(lo_done, 1)

            def normalise(g, b):
                at = (GB * g + b) if b < 3 else GB * g - 1
                dve.wait_ge(tail_full, tail_use(g, f"OT{b}") + 1)
                heads = tail[:, :].rearrange("p (s j w) -> p s j w", s=NS, j=NJ)
                vec.reciprocal(rl[:, :, :], heads[:, :, :, DK]).then_inc(norm_c, 1)
                dve.wait_ge(norm_c, at + 1)
                vec.tensor_tensor(a_sb[:, :].rearrange("p (j s d) -> p s j d", j=NJ, s=NS), heads[:, :, :, 0:DK],
                                  rl[:, :, :].unsqueeze(3).broadcast_to([P, NS, NJ, DK]), ALU.mult).then_inc(tail_free, 1)

            def residual(g, b, par):
                at = (GB * g + b) if b < 3 else GB * g - 1
                if b == 0:
                    dve.wait_ge(x_plus, g + 1)
                dve.wait_ge(tail_full, tail_use(g, f"y{b}") + 1)
                vec.scalar_tensor_tensor(x_all[:, at, :], tail[:, 0:D], gate[:, 0:1], x_all[:, at, :], ALU.mult, ALU.add).then_inc(tail_free, 1)
                dve.wait_ge(tail_free, tail_use(g, f"y{b}") + 1)
                stats = Chain(dve, ln2_stats, 2, at)
                apart(dve)
                stats.link(vec.bn_stats(st2[:, b, :], x_all[:, at, :]))
                apart(dve)
                stats.step(vec.bn_aggr(mv2[:, par, b, :], st2[:, b, :]))

            chains = {}

            def route_select(g):
                chains["now"] = c = Chain(dve, route_c, ROUTE, g - 1)
                dve.wait_ge(tail_full, tail_use(g, "logits") + 1)
                vec.tensor_tensor(lg[:, :, :], tail[:, 0:GB * E].rearrange("p (b e) -> p b e", b=GB),
                                  br_b[:, :].unsqueeze(1).broadcast_to([P, GB, E]), ALU.add).then_inc(tail_free, 1)
                dve.wait_ge(tail_free, tail_use(g, "logits") + 1)
                apart(dve)
                for b in range(GB):
                    last = vec.max(t8[:, b, :], lg[:, b, :])
                c.link(last)
                apart(dve)
                for b in range(GB):
                    last = vec.max_index(ti[:, b, :], t8[:, b, :], lg[:, b, :])
                c.step(last)
                c.step(vec.tensor_tensor(dz[:, :, :], t8[:, :, :], t8[:, :, 0:1].broadcast_to([P, GB, E]), ALU.subtract))
                assert c.count == R_DIFF

            def route_masks(g):
                c = chains["now"]
                c.settle()
                c.link(vec.tensor_copy(tif[:, :, :], ti[:, :, 0:TOPK]))
                for k in range(TOPK):
                    last = vec.tensor_tensor(mk[:, :, k, :], consts[:, C_IOTA:C_IOTA + E].unsqueeze(1).broadcast_to([P, GB, E]),
                                             tif[:, :, k:k + 1].broadcast_to([P, GB, E]), ALU.is_equal)
                c.link(last)
                c.link(vec.tensor_tensor(mboth[:, :, :], mk[:, :, 0, :], mk[:, :, 1, :], ALU.add))
                assert c.count == R_MASK
                c.step(vec.reduce_sum(msum[:, :], mboth[:, :, :].rearrange("p b e -> p e b"), AX_X))

            def route_weights(g, par):
                c = chains["now"]
                dve.wait_ge(ez_done, g)
                c.link(vec.reduce_sum(z1[:, :], ez[:, :, :], AX_X))
                c.link(vec.reciprocal(z2[:, :], z1[:, :]))
                c.link(vec.tensor_tensor(pk[:, :, :], ez[:, :, 0:TOPK], z2[:, :].unsqueeze(2).broadcast_to([P, GB, TOPK]), ALU.mult))
                c.link(vec.reduce_sum(z3[:, :], pk[:, :, :], AX_X))
                c.link(vec.tensor_scalar(z4[:, :], z3[:, :], MOE_EPS, None, ALU.add))
                c.link(vec.reciprocal(z5[:, :], z4[:, :]))
                c.link(vec.tensor_tensor(wk2[:, :, :], pk[:, :, :], z5[:, :].unsqueeze(2).broadcast_to([P, GB, TOPK]), ALU.mult))
                c.link(vec.reduce_sum(z6[:, :], wk2[:, :, :], AX_X))
                c.link(vec.tensor_scalar(z7[:, :], z6[:, :], MOE_EPS, None, ALU.add))
                c.link(vec.reciprocal(z8[:, :], z7[:, :]))
                c.step(vec.scalar_tensor_tensor(pay[:, par, :, :, D + 1], wk2[:, :, :], gate[:, 1:2], z8[:, :].unsqueeze(2).broadcast_to([P, GB, TOPK]),
                                                ALU.mult, ALU.mult))

            def route_slots(g, par):
                c = chains["now"]
                dve.wait_ge(tail_full, tail_use(g, "rank") + 1)
                vec.tensor_tensor(rank_b[:, :, :], tail[:, 0:GB * E].rearrange("p (b e) -> p b e", b=GB),
                                  consts[:, C_BASE:C_BASE + E].unsqueeze(1).broadcast_to([P, GB, E]), ALU.add).then_inc(tail_free, 1)
                dve.wait_ge(tail_free, tail_use(g, "rank") + 1)
                for k in range(TOPK):
                    last = vec.tensor_tensor(sel[:, :, k, :], mk[:, :, k, :], rank_b[:, :, :], ALU.mult)
                c.link(last)
                c.link(vec.reduce_sum(slot_f[:, :, :], sel[:, :, :, :], AX_X))
                c.step(vec.tensor_copy(slot_i[:, par, :], slot_f[:, :, :].rearrange("p b k -> p (b k)")))
                c.step(vec.tensor_tensor(mcarry[:, :], mcarry[:, :], msum[:, :], ALU.add))
                assert c.count == ROUTE

            def w1_low(g):
                dve.wait_ge(w1hi_done, g + 1)
                vec.scalar_tensor_tensor(w1_lo[:, g, :], w1_stage[:, :], W1_SCALE, w1_hi[:, g, :], ALU.mult, ALU.subtract).then_inc(w1lo_done, 1)

            def body(g, par, is_first, is_last, pairs):
                for u in range(UPG):
                    if u < UPG - 2:
                        maxima(g, u + 2)
                    elif not is_last:
                        maxima(g + 1, u + 2 - UPG)
                    if u == 1:
                        v_out(g, 3)
                        if not is_first:
                            normalise(g, 3)
                    if u == 3 and not is_first:
                        residual(g, 3, 1 - par)
                    if u == 4 and not is_last:
                        split_lo(g, "q", 0)
                    if u in (5, 9, 13):
                        if not is_last:
                            v_out(g, (u - 5) // 4)
                        normalise(g, (u - 5) // 4)
                    if u == 6 and not is_last:
                        split_lo(g, "k", 1)
                    if u in (7, 11, 15):
                        residual(g, (u - 7) // 4, par)
                    if u == 10:
                        w1_low(g)
                    if not is_first:
                        if u == 10:
                            route_select(g)
                        if u == 11:
                            route_masks(g)
                        if u == 12:
                            route_weights(g, 1 - par)
                        if u == 14:
                            route_slots(g, 1 - par)

            def stats1(first, end, n):
                for b in range(first, end):
                    last = vec.bn_stats(st1[:, b, :], x_all[:, b, :])
                last.then_inc(ln1_stats, 1)
                dve.wait_ge(ln1_stats, 2 * n + 1)
                for b in range(first, end):
                    last = vec.bn_aggr(mv1[:, b, :], st1[:, b, :])
                last.then_inc(ln1_stats, 1)

            dve.wait_ge(x_first, 16)
            stats1(0, GB, 0)
            vec.memset(ones[:, :], 1.0)
            vec.memset(mcarry[:, :], 0.0)
            vec.memset(ones8[:, :], 1.0).then_inc(setup, 1)
            vec.memset(diag["k"][:, 0].rearrange("p j s t -> p (j s t)").bitcast(U32), 0).then_inc(zeroed[0], 1)
            dve.wait_ge(w_in, 16 * 9)
            vec.tensor_scalar(neg_ident[:, :], ident[:, :], -1.0, None, ALU.mult).then_inc(setup, 1)
            dve.wait_ge(gates_done, 1)
            vec.tensor_scalar(gbo[:, :], bo_b[:, :], gate[:, 0:1], None, ALU.mult).then_inc(gbo_done, 1)
            dve.wait_ge(v_zeroed, 2)
            split_lo(-1, "q", 0)
            v_out(-1, 0)
            split_lo(-1, "k", 1)
            v_out(-1, 1)
            v_out(-1, 2)
            dve.wait_ge(x_rest, 16)
            stats1(GB, NB, 1)
            dve.wait_ge(w_in2, 16 * 8)
            vec.tensor_copy(tri[:, :], tri32[:, :]).then_inc(tri_done, 1)
            maxima(0, 0)
            maxima(0, 1)
            bodies(dve, body)
            normalise(NG, 3)
            residual(NG, 3, 1)
            route_select(NG)
            route_masks(NG)
            route_weights(NG, 1)
            route_slots(NG, 1)

            c = Chain(dve, table_c, TABLE, 0)
            dve.wait_ge(cnt_full, 1)
            c.link(vec.tensor_copy(cnt[:, :], tail[:, 0:E]))
            c.link(vec.tensor_tensor(fill_f[:, :], cnt[:, :], consts[:, C_BASE:C_BASE + E], ALU.add))
            c.step(vec.tensor_copy(fill_i[:, :], fill_f[:, :]))
            c.link(vec.tensor_tensor(over[:, :, :], cnt[:, :].unsqueeze(2).broadcast_to([P, E, MAXT]),
                                     consts[:, C_STEP:C_STEP + MAXT].unsqueeze(1).broadcast_to([P, E, MAXT]), ALU.is_gt))
            c.link(vec.reduce_sum(ntile[:, :], over[:, :, :], AX_X))
            c.link(vec.tensor_tensor_scan(ntile_end[:, :], ones8[:, :], ntile[:, :], 0.0, ALU.mult, ALU.add))
            tiles_c = consts[:, C_TILE:C_TILE + NT]
            c.link(vec.tensor_tensor(past[:, :, :], tiles_c.unsqueeze(2).broadcast_to([P, NT, E]),
                                     ntile_end[:, :].unsqueeze(1).broadcast_to([P, NT, E]), ALU.is_ge))
            c.step(vec.reduce_sum(te[:, :], past[:, :, :], AX_X))
            c.link(vec.tensor_tensor(pastn[:, :, :], past[:, :, :], ntile[:, :].unsqueeze(1).broadcast_to([P, NT, E]), ALU.mult))
            c.link(vec.reduce_sum(tprev[:, :], pastn[:, :, :], AX_X))
            c.link(vec.tensor_tensor(ta[:, :], tiles_c, tprev[:, :], ALU.subtract))
            c.link(vec.tensor_scalar(tb[:, :], te[:, :], float(RS), None, ALU.mult))
            c.link(vec.scalar_tensor_tensor(tr[:, :], ta[:, :], float(TR), tb[:, :], ALU.mult, ALU.add))
            c.step(vec.tensor_scalar(tile_row[:, :], tr[:, :], float(E * RS), None, ALU.min))
            c.link(vec.tensor_scalar(tile_e[:, :], te[:, :], float(E - 1), None, ALU.min))

            def x_lo(i, r):
                dve.wait_ge(xh_done, i + 1)
                vec.tensor_tensor(xl[:, r, :], xT_bank[:, 0:TR], xh[:, r, :], ALU.subtract).then_inc(xl_done, 1)
                wait(dve, ys_done, i - PING + 1)
                vec.tensor_copy(meta[:, r], xt[:, r, :, D:PW]).then_inc(taken, 1)

            def y_end(i, r, turn):
                e = dve.value_load(tile_e[0:1, i:i + 1] if isinstance(i, int) else tile_e[0:1, bass.ds(i, 1)], min_val=0, max_val=E - 1)
                dve.wait_ge(y_full, i + 1)
                vec.tensor_tensor(yb[:, r], y_bank[:, 0:2 * D].rearrange("p (h d) -> p h d", h=2),
                                  b2_b[:, e, :].unsqueeze(1).broadcast_to([P, 2, D]), ALU.add).then_inc(yb_done, 1)
                dve.wait_ge(yb_done, i + 1)
                dve.wait_ge(taken, i + 1)
                wait(dve, y_tile[r], 32 * turn)
                for h in range(2):
                    vec.tensor_scalar(ys[:, r, h, :], yb[:, r, h, :], meta[:, r, h, 1:2], None, ALU.mult)
                vec.tensor_copy(dest[:, r, :], meta[:, r, :, 0]).then_inc(ys_done, 1)

            x_lo(0, 0)
            x_lo(1, 1)

            def tiles(n, is_last):
                for r in range(PING):
                    i = n * PING + r
                    if not (is_last and r >= PING - 2):
                        x_lo(i + 2, (r + 2) % PING)
                    y_end(i, r, n)

            tiles(0, False)
            with dve.Fori(1, NT // PING - 1) as n:
                tiles(n, False)
            tiles(NT // PING - 1, True)

            for g in range(NG):
                r = g % 2
                dve.wait_ge(y_ready[r], 16 * TOPK * (g // 2 + 1))
                wait(dve, out_done[r], 16 * (g // 2))
                s = Chain(dve, sum_c, 2, g)
                s.link(vec.tensor_tensor(res[:, r], y_in[:, r, 0], y_in[:, r, 1], ALU.add))
                s.step(vec.tensor_tensor(res[:, r], res[:, r], x_all[:, g * GB:(g + 1) * GB, :], ALU.add))

        @block.gpsimd
        def _(pool):
            gp = nc.gpsimd

            def rstd(sem_, n, rs, nb, mv, k):
                c = Chain(pool, sem_, RSTEPS, n)
                apart(pool)
                c.link(gp.tensor_scalar(rs, mv[:, :, 1], LN_EPS, 1.0, ALU.add, ALU.mult))
                c.link(gp.tensor_tensor(rs, rs, neg_half[:, 0:k], ALU.pow))
                apart(pool)
                c.link(gp.tensor_scalar(nb, mv[:, :, 0], -1.0, 0.0, ALU.mult, ALU.add))
                c.step(gp.tensor_tensor(nb, nb, rs, ALU.mult))

            def add_bias(g):
                pool.wait_ge(ln1_done, g + 2)
                apart(pool)
                x4 = x_all[:, bass.ds(g * GB + GB, GB), :]
                gp.tensor_tensor(x4, x4, gbo[:, :].unsqueeze(1).broadcast_to([P, GB, D]), ALU.add).then_inc(x_plus, 1)

            def rstd2(g, par):
                pool.wait_ge(ln2_stats, 2 * GB * g)
                rstd(ln2_rs, g - 1, rs2[:, :], nb2[:, :], mv2[:, par], GB)

            def scatter(g, par, pairs):
                pool.wait_ge(ln2_done, g)
                apart(pool)
                ids = consts[:, bass.ds((g - 1) * (GB * TOPK) + C_ID, GB * TOPK)]
                gp.tensor_copy(pay[:, par, :, :, D],
                               ids.rearrange("p (b k) -> p b k", b=GB)).then_inc(ids_done, 1)
                pool.wait_ge(ids_done, g)
                pool.wait_ge(route_c, ROUTE * g)
                apart(pool)
                for b in range(GB):
                    for k in range(TOPK):
                        gp.indirect_dma_start(out=rows_dram, out_offset=bass.IndirectOffsetOnAxis(ap=slot_i[:, par, b * TOPK + k:b * TOPK + k + 1], axis=0),
                                              in_=pay[:, par, b, k, :], in_offset=None).then_inc(scattered[par], 16)
                pool.wait_ge(scattered[par], 16 * GB * TOPK * (pairs + 1))

            def body(g, par, is_first, is_last, pairs):
                if not is_last:
                    add_bias(g)
                if not is_first:
                    rstd2(g, 1 - par)
                    scatter(g, 1 - par, pairs)

            gp.memset(neg_half[:, :], -0.5).then_inc(setup_pool, 1)
            pool.wait_ge(setup_pool, 1)
            pool.wait_ge(ln1_stats, 2)
            rstd(ln1_rs, 0, rs1[:, 0:GB], nb1[:, 0:GB], mv1[:, 0:GB], GB)
            gp.memset(v_aug[:, :, :, :], 0.0).then_inc(v_zeroed, 1)
            pool.wait_ge(v_zeroed, 1)
            gp.memset(v_aug[:, :, :, DK], 1.0).then_inc(v_zeroed, 1)
            gp.memset(diag["q"][:, 0].rearrange("p j s t -> p (j s t)").bitcast(U32), 0).then_inc(zeroed[0], 1)
            pool.wait_ge(gbo_done, 1)
            pool.wait_ge(ln1_stats, 4)
            rstd(ln1_rs, 1, rs1[:, GB:NB], nb1[:, GB:NB], mv1[:, GB:NB], NB - GB)
            add_bias(-1)
            for t in "kq":
                gp.memset(diag[t][:, 1].rearrange("p j s t -> p (j s t)").bitcast(U32), 0).then_inc(zeroed[1], 1)
            gp.memset(pad[:, :, :], 0.0).then_inc(pad_done, 1)
            pool.wait_ge(pad_done, 1)
            gp.memset(pad[:, :, D], NOWHERE).then_inc(pad_done, 1)
            bodies(pool, body)
            rstd2(NG, 1)
            scatter(NG, 1, NG // 2 - 1)

            def put(i, r):
                pool.wait_ge(ys_done, i + 1)
                apart(pool)
                for h in range(2):
                    gp.indirect_dma_start(out=y_dram, out_offset=bass.IndirectOffsetOnAxis(ap=dest[:, r, h:h + 1], axis=0), in_=ys[:, r, h, :],
                                          in_offset=None, bounds_check=TOPK * NTOK - 1, oob_is_err=False).then_inc(y_tile[r], 16)

            with pool.Fori(0, NT // PING) as n:
                for r in range(PING):
                    put(n * PING + r, r)


_INS = ['x', 'ctx_in', 'gates', 'wq', 'bq', 'wk', 'bk', 'wv', 'bv', 'wo', 'bo', 'wr', 'br', 'w1', 'b1', 'w2', 'b2', 'ident', 'tri', 'consts']


def kernel(**inputs):
    import concourse.bacc as _bacc
    from concourse.bass_utils import run_bass_kernel_spmd as _run

    a = {k: np.asarray(v) for k, v in inputs.items()}

    def by_block(w):
        return w.reshape(w.shape[:-1] + (NJ, NS, DK)).swapaxes(-1, -2).reshape(w.shape)

    consts = np.zeros(C_END, np.float32)
    consts[C_IOTA:C_IOTA + E] = np.arange(E)
    consts[C_BASE:C_BASE + E] = np.arange(E) * RS
    consts[C_TILE:C_TILE + NT] = np.arange(NT)
    consts[C_STEP:C_STEP + MAXT] = np.arange(MAXT) * TR
    consts = np.tile(consts, (P, 1))
    token = np.arange(NB)[None, :, None] * P + np.arange(P)[:, None, None]
    consts[:, C_ID:] = (token + np.arange(TOPK)[None, None, :] * NTOK).reshape(P, NB * TOPK)
    host = {
        'x': a['x'], 'ctx_in': a['ctx_1024'], 'gates': np.concatenate([a['g_xattn'], a['g_ffn']]),
        'wq': by_block(a['L0_xattn_W_q'].T), 'bq': by_block(a['L0_xattn_b_q'])[:, None],
        'wk': by_block(a['L0_xattn_W_k'].T), 'bk': by_block(a['L0_xattn_b_k'])[:, None],
        'wv': a['L0_xattn_W_v'].T, 'bv': a['L0_xattn_b_v'], 'wo': a['L0_xattn_W_o'].T, 'bo': a['L0_xattn_b_o'],
        'wr': a['L0_ffn_Wr'], 'br': a['L0_ffn_br'], 'w1': a['L0_ffn_W1'],
        'b1': a['L0_ffn_b1'].reshape(E * MC, P).T,
        'w2': a['L0_ffn_W2'].reshape(E * MC, P, D).transpose(1, 0, 2), 'b2': a['L0_ffn_b2'],
        'ident': np.eye(P, dtype=np.float32), 'tri': np.triu(np.ones((P, P), np.float32), 1), 'consts': consts,
    }
    nc = _bacc.Bacc("TRN2", target_bir_lowering=False, num_devices=1)
    arrays, args = {}, []
    for name in _INS:
        v = np.ascontiguousarray(host[name])
        arrays["in_" + name] = v
        args.append(nc.dram_tensor("in_" + name, v.shape, mybir.dt.from_np(v.dtype), kind="ExternalInput").ap())
    args.append(nc.dram_tensor("out", (NB, P, D), F32, kind="ExternalOutput").ap())
    moe_attention(nc, *args)
    r = _run(nc, [arrays], core_ids=[0])
    return r.results[0]["out"]
```

```python
from contextlib import ExitStack

import numpy as np

import concourse.bass as bass
from concourse import mybir

ALU = mybir.AluOpType
ACT = mybir.ActivationFunctionType
AX_X = mybir.AxisListType.X
F32 = mybir.dt.float32
F16 = mybir.dt.float16
BF16 = mybir.dt.bfloat16
I32 = mybir.dt.int32
U32 = mybir.dt.uint32

P = 128
NB = 32
D = 128
NH, DK = 16, 8
NJ, NS = 4, 4
GB = 4
NG = NB // GB
GT = GB * P
UPG = GB * NS
E, M, TOPK = 8, 512, 2
MC = M // P
NTOK = NB * P
TR = 256
NT = (TOPK * NTOK + E * (TR - 1)) // TR
RS = NTOK + TR
ROWS = E * RS + TR
PW = D + 1
MAXT = NTOK // TR
LN_EPS, MOE_EPS = 1e-5, 1e-9
W_SCALE = 64.0
NOWHERE = float(4 * NTOK)
PING = 3
TURNS = NT // PING
AHEAD = PING + 2
ROW = 8

C_IOTA, C_BASE, C_TILE, C_STEP, C_ID = 0, E, 2 * E, 2 * E + TURNS * AHEAD, 2 * E + TURNS * AHEAD + MAXT
C_END = C_ID + NB * TOPK


def wait(eng, sem, value):
    if isinstance(value, int) and value <= 0:
        return
    eng.wait_ge(sem, value)


class Chain:

    def __init__(self, eng, sem, per, n):
        self.eng, self.sem, self.per, self.n, self.count = eng, sem, per, n, 0

    def step(self, ins):
        self.count += 1
        assert self.count <= self.per
        ins.then_inc(self.sem, 1)

    def settle(self):
        self.eng.wait_ge(self.sem, self.n * self.per + self.count)

    def link(self, ins):
        self.step(ins)
        self.settle()


def moe_attention(nc, x, ctx_in, gates, wq, bq, wk, bk, wv, bv, wo, bo, wr, br, w1, b1, w2, b2, ident_in, tri_in, consts_in, out):
    bounce = {t: nc.dram_tensor(f"bounce_{t}", (NJ, 4, DK, NS, GT), F16, kind="Internal").ap() for t in "qk"}
    rows_dram = nc.dram_tensor("rows_dram", (ROWS, PW), F32, kind="Internal").ap()
    y_dram = nc.dram_tensor("y_dram", (TOPK * NTOK, D), F32, kind="Internal").ap()

    with ExitStack() as stack:
        def sb(name, shape, dt=F32):
            return stack.enter_context(nc.sbuf_tensor(name, shape, dt))

        def psum(name, shape):
            return stack.enter_context(nc.psum_tensor(name, shape, F32))

        def sem(name):
            return stack.enter_context(nc.semaphore(name))

        ident = sb("ident", [P, P])
        neg_ident = sb("neg_ident", [P, P], BF16)
        tri32 = sb("tri32", [P, P])
        tri = sb("tri", [P, P], BF16)
        ones = sb("ones", [P, P], BF16)
        consts = sb("consts", [P, C_END])
        gate_in = sb("gate_in", [P, 2])
        gate = sb("gate", [P, 2])
        neg_half = sb("neg_half", [P, NB])
        wqT, wkT, wvT, woT = (sb(n, [P, D]) for n in ("wqT", "wkT", "wvT", "woT"))
        bq_c, bk_c = sb("bq_c", [P, 1]), sb("bk_c", [P, 1])
        bv_b, bo_b, gbo = sb("bv_b", [P, D]), sb("bo_b", [P, D]), sb("gbo", [P, D])
        wr_sb, br_b = sb("wr_sb", [P, E]), sb("br_b", [P, E])
        w1_stage = sb("w1_stage", [P, M])
        w1_hi, w1_lo = sb("w1_hi", [P, E, M], F16), sb("w1_lo", [P, E, M], F16)
        b1_c = sb("b1_c", [P, E, MC])
        w2_stage = sb("w2_stage", [P, MC * D])
        w2_hi, w2_lo = sb("w2_hi", [P, E, MC * D], F16), sb("w2_lo", [P, E, MC * D], F16)
        b2_b = sb("b2_b", [P, E, D])
        x_all = sb("x_all", [P, NB, D])
        c_in = sb("c_in", [P, GB, D])
        xn = sb("xn", [P, GB, D])
        st1, mv1, rs1, nb1 = sb("st1", [P, NB, 6]), sb("mv1", [P, NB, 2]), sb("rs1", [P, NB]), sb("nb1", [P, NB])
        st2, mv2, rs2, nb2 = sb("st2", [P, GB, 6]), sb("mv2", [P, 2, GB, 2]), sb("rs2", [P, GB]), sb("nb2", [P, GB])
        xnT, cT = sb("xnT", [P, GT]), sb("cT", [P, GT])
        parts = {t: sb(f"parts_{t}", [P, 2, GT], F16) for t in "qk"}
        plain = {t: sb(f"plain_{t}", [P, 2, NS, GT], F16) for t in "qk"}
        diag = {t: sb(f"diag_{t}", [P, 2, NJ, NS, GT], F16) for t in "qk"}
        v_aug = sb("v_aug", [P, GB, NH, 32])
        maxes = sb("maxes", [P, UPG, NJ], BF16)
        probs = sb("probs", [P, 4, NJ, P])
        o_sb = sb("o_sb", [P, NS * P])
        rl = sb("rl", [P, NS, NJ])
        a_sb, aT = sb("a_sb", [P, D]), sb("aT", [P, P])
        pay = sb("pay", [P, 2, GB, TOPK, PW])
        x2T = sb("x2T", [P, GT])
        lg, t8 = sb("lg", [P, GB, E]), sb("t8", [P, GB, E])
        ti = sb("ti", [P, GB, E], U32)
        mk, mboth = sb("mk", [P, GB, TOPK, E]), sb("mboth", [P, GB, E], BF16)
        mcarry, msum = sb("mcarry", [P, E], BF16), sb("msum", [P, E])
        t8_all, dz, ez = (sb(n, [P, NB, E]) for n in ("t8_all", "dz", "ez"))
        z1, z2, z3, z4, z5, z6, z7, z8 = (sb(f"z{i}", [P, NB]) for i in range(8))
        pk, wk2, weight = (sb(n, [P, NB, TOPK]) for n in ("pk", "wk2", "weight"))
        rank_b, sel, slot_f = sb("rank_b", [P, GB, E]), sb("sel", [P, GB, TOPK, E]), sb("slot_f", [P, GB, TOPK])
        slot_i = sb("slot_i", [P, 2, GB * TOPK], I32)
        cnt, fill_f, fill_i = sb("cnt", [P, E]), sb("fill_f", [P, E]), sb("fill_i", [P, E], I32)
        over, ntile, ntile_end = sb("over", [P, E, MAXT]), sb("ntile", [P, E]), sb("ntile_end", [P, E])
        past, pastn = sb("past", [P, TURNS * AHEAD, E]), sb("pastn", [P, TURNS * AHEAD, E])
        te, tprev, ta, tb, tr = (sb(n, [P, TURNS * AHEAD]) for n in ("te", "tprev", "ta", "tb", "tr"))
        tile_row, tile_e = sb("tile_row", [P, TURNS, ROW], I32), sb("tile_e", [P, TURNS, ROW], I32)
        pad = sb("pad", [P, 2, PW])
        gelu_warm = sb("gelu_warm", [P, 1])
        ones8 = sb("ones8", [P, E])
        xt = sb("xt", [P, PING, 2, PW])
        xh, xl = sb("xh", [P, PING, TR], F16), sb("xl", [P, PING, TR], F16)
        room_h = diag["k"][:, :, :, :, :].rearrange("p a j s t -> p (a j s t)")
        n_h = PING * MC * TR
        hT = room_h[:, 0:2 * n_h].bitcast(F32).rearrange("p (r m) -> p r m", r=PING)
        h_hi = room_h[:, 2 * n_h:3 * n_h].rearrange("p (r m) -> p r m", r=PING)
        h_lo = room_h[:, 3 * n_h:4 * n_h].rearrange("p (r m) -> p r m", r=PING)
        yb = plain["k"][:, :, :, :].rearrange("p a s t -> p (a s t)").bitcast(F32)[:, 0:PING * 2 * D].rearrange("p (r h d) -> p r h d", r=PING, h=2)
        row_ids, dest = sb("row_ids", [P, PING, 2]), sb("dest", [P, PING, 2], I32)
        y_in = diag["q"][:, :, :, :, :].rearrange("p a j s t -> p (a j s t)").bitcast(F32).rearrange("p (r k b d) -> p r k b d", r=NG, k=TOPK, b=GB)

        s_bank = [psum(f"s_bank{i}", [P, 512]) for i in range(2)]
        t_bank = [psum(f"t_bank{i}", [P, 512]) for i in range(2)]
        o_bank = [psum(f"o_bank{i}", [P, 512]) for i in range(2)]
        prep = psum("prep", [P, 512])
        tail = psum("tail", [P, 512])
        h_bank = [[s_bank[0], s_bank[1]], [t_bank[0], t_bank[1]], [o_bank[0], o_bank[1]]]
        xT_bank, y_bank = prep, tail

        x_first, x_second, x_rest, ident_here, wk_here, wq_here, w_in, w_in2 = (sem(n) for n in ("x_first", "x_second", "x_rest", "ident_here", "wk_here", "wq_here", "w_in", "w_in2"))
        c_ready, w1_ready, ffn_in = sem("c_ready"), sem("w1_ready"), sem("ffn_in")
        bounced = {t: sem(f"bounced_{t}") for t in "qk"}
        spread = {t: sem(f"spread_{t}") for t in "qk"}
        scattered, filled = [sem(f"scattered{i}") for i in range(2)], sem("filled")
        setup, gates_done, zeroed = sem("setup"), sem("gates_done"), {t: [sem(f"zeroed_{t}{i}") for i in range(2)] for t in "qk"}
        tri_done, pad_done, v_zeroed = sem("tri_done"), sem("pad_done"), sem("v_zeroed")
        gbo_done, half_done = sem("gbo_done"), sem("half_done")
        prep_full, v_done, xc_done = sem("prep_full"), sem("v_done"), sem("xc_done")
        tail_full, tail_free = sem("tail_full"), sem("tail_free")
        scored, maxed, scoredT, exped, pv_done, o_out = (sem(n) for n in ("scored", "maxed", "scoredT", "exped", "pv_done", "o_out"))
        ln1_stats, ln1_rs, ln1_done, x_plus = (sem(n) for n in ("ln1_stats", "ln1_rs", "ln1_done", "x_plus"))
        ln2_stats, ln2_rs, ln2_done = (sem(n) for n in ("ln2_stats", "ln2_rs", "ln2_done"))
        hi_done, lo_done = sem("hi_done"), sem("lo_done")
        norm_c, x2T_done, lg_done, route_c, ids_done = (sem(n) for n in ("norm_c", "x2T_done", "lg_done", "route_c", "ids_done"))
        dz_done, ez_done, weight_c, kept, warm = (sem(n) for n in ("dz_done", "ez_done", "weight_c", "kept", "warm"))
        w1hi_done, w1lo_done = sem("w1hi_done"), sem("w1lo_done")
        w2_ready, w2hi_done, w2lo_done = sem("w2_ready"), sem("w2hi_done"), sem("w2lo_done")
        cnt_full, table_c = sem("cnt_full"), sem("table_c")
        taken = sem("taken")
        x_tile = [sem(f"x_tile{i}") for i in range(PING)]
        y_tile = [sem(f"y_tile{i}") for i in range(PING)]
        xT_full, xh_done, xl_done = sem("xT_full"), sem("xh_done"), sem("xl_done")
        h_full, h_done, hhi_done, hlo_done, y_full, yb_done, dest_done = (sem(n) for n in ("h_full", "h_done", "hhi_done", "hlo_done", "y_full", "yb_done", "dest_done"))
        y_ready = [sem(f"y_ready{i}") for i in range(NG)]
        sum_c = sem("sum_c")
        out_done = sem("out_done")
        RSTEPS, ROUTE, WSTEPS, TABLE = 4, 9, 11, 15
        T_FILL = 3
        R_MAX, R_INDEX, R_MASK, R_BOTH, R_SUM, R_SEL, R_SLOT, R_SLOT_I, R_CARRY = range(1, ROUTE + 1)

        PREP = ("V3", "cT", "xT", "K", "Q", "V0", "V1", "x2T", "logits", "V2", "rank")
        ROUTING = ("x2T", "logits", "rank")
        TAIL = tuple(w + str(b) for b in (3, 0, 1, 2) for w in ("OT", "aT", "y"))

        def prep_uses(g):
            if not isinstance(g, int) or 0 < g < NG - 1:
                return PREP
            if g == -1:
                return ("cT", "K", "xT", "Q", "V0", "V1", "V2")
            if g == 0:
                return tuple(w for w in PREP if w not in ROUTING)
            return ("V3",) + ROUTING if g == NG - 1 else ROUTING

        def prep_use(g, what):
            uses = prep_uses(g)
            if isinstance(g, int) and g < 1:
                return 7 * (g + 1) + uses.index(what)
            base = 15 + 11 * (NG - 2) + 4 if isinstance(g, int) and g == NG else g * 11 + 4
            return base + uses.index(what)

        def bank_of(g, what):
            own = {"cT": t_bank[1], "Q": s_bank[0], "K": s_bank[1], "V0": o_bank[0], "V1": o_bank[1]}
            return own.get(what, prep) if isinstance(g, int) and g < 0 else prep

        def prep_done(g, what):
            if what[0] == "V":
                return v_done, 4 * g + 4 + ("V3", "V0", "V1", "V2").index(what)
            if what in ("cT", "xT"):
                return xc_done, 2 * g + 3 + (what == "xT")
            if what in ("Q", "K"):
                return lo_done, 2 * g + 3 + (what == "Q")
            if what == "x2T":
                return x2T_done, g
            return lg_done, 2 * g + 1 + (what == "rank")

        def tail_use(g, what):
            return g * 12 - 3 + TAIL.index(what)

        def bodies(eng, body):
            body(0, 0, True, False, 0)
            with eng.Fori(0, (NG - 2) // 2) as n:
                body(n * 2 + 1, 1, False, False, n)
                body(n * 2 + 2, 0, False, False, n)
            body(NG - 1, 1, False, True, NG // 2 - 1)

        waited = {e: sem(f"waited_{n}") for n, e in (("sp", nc.sync.engine), ("act", nc.scalar.engine), ("dve", nc.vector.engine), ("pool", nc.gpsimd.engine))}

        def apart(eng):
            eng.sem_inc(waited[eng.engine], 1)

        def load_row(eng, table, n, first, end, max_val):
            row = table[0:1, n, first:end] if isinstance(n, int) else table[0:1, bass.ds(n, 1), first:end].rearrange("p n k -> p (n k)")
            _, values = nc.values_load_multi_w_load_instructions(row, engines=[eng.engine], min_val=0, max_val=max_val)
            return values

        block = stack.enter_context(nc.Block())

        @block.sync
        def _(sp):
            xv = x.rearrange("b p d -> p b d")
            cv = ctx_in.rearrange("b p d -> p b d")
            sp.dma_start(c_in[:, :, :], cv[:, 0:GB, :]).then_inc(c_ready, 16)
            sp.dma_start(x_all[:, 0:GB, :], xv[:, 0:GB, :]).then_inc(x_first, 16)
            small = [(ident[:, :], ident_in, ident_here), (wkT[:, :], wk, wk_here), (bk_c[:, :], bk, wk_here), (wqT[:, :], wq, wq_here), (bq_c[:, :], bq, wq_here),
                     (wvT[:, :], wv, w_in), (bv_b[:, :], bv.partition_broadcast(P), w_in), (gate_in[:, :], gates.partition_broadcast(P), w_in),
                     (bo_b[:, :], bo.partition_broadcast(P), w_in)]
            for dst, src, here in small:
                sp.dma_start(dst, src).then_inc(here, 16)
            sp.dma_start(x_all[:, GB:2 * GB, :], xv[:, GB:2 * GB, :]).then_inc(x_second, 16)
            late = [(woT[:, :], wo), (wr_sb[:, :], wr), (br_b[:, :], br.partition_broadcast(P)), (tri32[:, :], tri_in),
                    (consts[:, :], consts_in)]
            for dst, src in late:
                sp.dma_start(dst, src).then_inc(w_in2, 16)

            def bounce_part(G, t, n):
                wait(sp, lo_done, 2 * G + n + 1)
                apart(sp)
                wait(sp, spread[t], 16 * 5 * G)
                for r in range(4):
                    part = r >> 1 if t == "q" else r & 1
                    sp.dma_start(bounce[t][:, r].rearrange("j i s t -> j (i s) t"), parts[t][:, part, :]).then_inc(bounced[t], 16)

            def spread_part(G, par, t):
                sp.wait_ge(bounced[t], 16 * 4 * (G + 1))
                apart(sp)
                wait(sp, scoredT, UPG * (G - 1))
                sp.wait_ge(zeroed[t][par], 1)
                sp.dma_start(plain[t][:, par], bounce[t].rearrange("j r i s t -> (j r i) s t")).then_inc(spread[t], 16)
                for j in range(NJ):
                    sp.dma_start(diag[t][32 * j:32 * j + 32, par, j], bounce[t][j].rearrange("r i s t -> (r i) s t")).then_inc(spread[t], 16)

            def body(g, par, is_first, is_last, pairs):
                if not is_last:
                    sp.wait_ge(*prep_done(g - 1, "cT"))
                    apart(sp)
                    sp.dma_start(c_in[:, :, :], cv[:, bass.ds(g * GB + GB, GB), :]).then_inc(c_ready, 16)
                wait(sp, w1lo_done, g)
                sp.dma_start(w1_stage[:, :], w1[g]).then_inc(w1_ready, 16)
                wait(sp, w2lo_done, g)
                sp.dma_start(w2_stage[:, :], w2[g]).then_inc(w2_ready, 16)
                if is_last:
                    for dst, src in [(b1_c[:, :, :].rearrange("p e c -> p (e c)"), b1), (b2_b[:, :, :], b2.partition_broadcast(P))]:
                        sp.dma_start(dst, src).then_inc(ffn_in, 16)
                    return
                if is_first:
                    sp.dma_start(x_all[:, 2 * GB:NB, :], xv[:, 2 * GB:NB, :]).then_inc(x_rest, 16)
                for n, t in enumerate("kq"):
                    bounce_part(g + 1, t, n)
                for t in "kq":
                    spread_part(g + 1, 1 - par, t)

            bounce_part(0, "k", 0)
            bounce_part(0, "q", 1)
            spread_part(0, 0, "k")
            spread_part(0, 0, "q")
            bodies(sp, body)

            sp.wait_ge(table_c, T_FILL)
            for e in range(0, E, 2):
                at = sp.value_load(fill_i[0:1, e:e + 1], min_val=e * RS, max_val=e * RS + NTOK)
                sp.dma_start(rows_dram[bass.ds(at, TR), :].rearrange("(p h) c -> p h c", h=2), pad[:, :, :]).then_inc(filled, 16)
            sp.wait_ge(filled, 16 * E)
            sp.wait_ge(table_c, TABLE)
            for i in range(2):
                sp.wait_ge(scattered[i], 16 * GB * TOPK * NG // 2 + 16)

            def load_tile(i, r, at):
                wait(sp, taken, i - PING + 1)
                apart(sp)
                sp.dma_start(xt[:, r], rows_dram[bass.ds(at, TR), :].rearrange("(p h) c -> p h c", h=2)).then_inc(x_tile[r], 16)

            at = load_row(sp, tile_row, 0, 0, PING, E * RS)
            for r in range(PING):
                load_tile(r, r, at[r])
            with sp.Fori(1, TURNS) as n:
                at = load_row(sp, tile_row, n, 0, PING, E * RS)
                for r in range(PING):
                    load_tile(n * PING + r, r, at[r])

            for r in range(PING):
                sp.wait_ge(y_tile[r], 32 * (TURNS))
            yv = y_dram.rearrange("(k b p) d -> k p b d", k=TOPK, p=P)
            for g in range(NG):
                for k in range(TOPK):
                    sp.dma_start(y_in[:, g, k], yv[k][:, g * GB:(g + 1) * GB, :]).then_inc(y_ready[g], 16)
            sp.wait_ge(out_done, 16 * NG)

        @block.tensor
        def _(pe):
            def prep_begin(g, what):
                uses = prep_uses(g)
                if isinstance(g, int) and g < 0:
                    if what == "V2":
                        pe.wait_ge(*prep_done(g, "xT"))
                elif what != uses[0]:
                    pe.wait_ge(*prep_done(g, uses[uses.index(what) - 1]))
                else:
                    if not (isinstance(g, int) and g == NG):
                        pe.wait_ge(*prep_done(g - 1, "V2"))
                    if not (isinstance(g, int) and g == 0):
                        pe.wait_ge(*prep_done(g - 1, "rank"))

            def tail_begin(g, what):
                wait(pe, tail_free, tail_use(g, what))

            def scores(g, par, u):
                if u == 0:
                    for t in "qk":
                        pe.wait_ge(spread[t], 16 * 5 * (g + 1))
                wait(pe, maxed, UPG * g + u - 1)
                b, s = u // NS, u % NS
                toks = slice(b * P, (b + 1) * P)
                nc.tensor.matmul(s_bank[u % 2][:, :], plain["q"][:, par, s, toks], diag["k"][:, par, :, s, toks],
                                 start=True, stop=True).then_inc(scored, 1)

            def scores_T(g, par, u):
                b, s = u // NS, u % NS
                toks = slice(b * P, (b + 1) * P)
                bank = t_bank[u % 2]
                wait(pe, exped, UPG * g + u - 1)
                nc.tensor.matmul(bank[:, :], plain["k"][:, par, s, toks], diag["q"][:, par, :, s, toks], start=True, stop=False,
                                 skip_group_check=True)
                pe.wait_ge(maxed, UPG * g + u + 1)
                for j in range(NJ):
                    last = nc.tensor.matmul(bank[:, j * P:(j + 1) * P], maxes[:, u, j:j + 1].broadcast_to([P, P]), neg_ident[:, :],
                                            start=False, stop=True, skip_group_check=True)
                last.then_inc(scoredT, 1)

            def values(g, u):
                if u < 0:
                    g, u = g - 1, UPG - 1
                b, s = u // NS, u % NS
                pe.wait_ge(exped, UPG * g + u + 1)
                if s == 0:
                    what = f"V{b}"
                    wait(pe, *prep_done(g if b == 3 else g - 1, what))
                    wait(pe, o_out, GB * g + b - 1)
                for j in range(NJ):
                    last = nc.tensor.matmul(o_bank[b % 2][32 * j:32 * j + 32, s * P:(s + 1) * P], v_aug[:, b, NJ * j + s, :],
                                            probs[:, u % 4, j, :], start=True, stop=True)
                last.then_inc(pv_done, 1)

            def project_v(g, b):
                prep_begin(g, f"V{b}")
                nc.tensor.matmul(bank_of(g, f"V{b}")[:, 0:D], cT[:, b * P:(b + 1) * P], wvT[:, :], start=True, stop=True).then_inc(prep_full, 1)

            def transpose4(bank, src):
                for b in range(GB):
                    last = nc.tensor.transpose(bank[:, b * P:(b + 1) * P], src(b), ident[:, :])
                return last

            def prep_x(g):
                prep_begin(g, "xT")
                pe.wait_ge(ln1_done, g + 2)
                transpose4(bank_of(g, "xT"), lambda b: xn[:, b, :]).then_inc(prep_full, 1)

            def prep_c(g):
                prep_begin(g, "cT")
                pe.wait_ge(c_ready, 16 * (g + 2))
                transpose4(bank_of(g, "cT"), lambda b: c_in[:, b, :]).then_inc(prep_full, 1)

            def prep_q(g):
                prep_begin(g, "Q")
                pe.wait_ge(*prep_done(g, "xT"))
                nc.tensor.matmul(bank_of(g, "Q")[:, :], wqT[:, :], xnT[:, :], start=True, stop=True).then_inc(prep_full, 1)

            def prep_k(g):
                prep_begin(g, "K")
                pe.wait_ge(*prep_done(g, "cT"))
                nc.tensor.matmul(bank_of(g, "K")[:, :], wkT[:, :], cT[:, :], start=True, stop=True).then_inc(prep_full, 1)

            def o_T(g, b):
                tail_begin(g, f"OT{b}")
                pe.wait_ge(o_out, GB * g + (b + 1 if b < 3 else 0))
                transpose4(tail, lambda s: o_sb[:, s * P:(s + 1) * P]).then_inc(tail_full, 1)

            def a_T(g, b):
                tail_begin(g, f"aT{b}")
                nc.tensor.transpose(tail[:, 0:P], a_sb[:, :], ident[:, :]).then_inc(tail_full, 1)

            def y_out(g, b):
                tail_begin(g, f"y{b}")
                nc.tensor.matmul(tail[:, 0:D], aT[:, :], woT[:, :], start=True, stop=True).then_inc(tail_full, 1)

            def x2_T(g, par):
                prep_begin(g, "x2T")
                pe.wait_ge(ln2_done, g)
                transpose4(prep, lambda b: pay[:, par, b, 0, 0:D]).then_inc(prep_full, 1)

            def logits(g):
                prep_begin(g, "logits")
                pe.wait_ge(x2T_done, g)
                for b in range(GB):
                    last = nc.tensor.matmul(prep[:, b * E:(b + 1) * E], x2T[:, b * P:(b + 1) * P], wr_sb[:, :], start=True, stop=True)
                last.then_inc(prep_full, 1)

            def rank(g):
                prep_begin(g, "rank")
                pe.wait_ge(route_c, ROUTE * (g - 1) + R_BOTH)
                out4 = prep[:, 0:GB * E].rearrange("p (b e) -> p b e", b=GB)
                nc.tensor.matmul(out4, tri[:, :], mboth[:, :, :], start=True, stop=False, skip_group_check=True)
                for k in range(1, GB):
                    nc.tensor.matmul(out4[:, k:GB, :], ones[:, :], mboth[:, 0:GB - k, :], start=False, stop=False, skip_group_check=True)
                nc.tensor.matmul(out4, ones[:, :], mcarry[:, :].unsqueeze(1).broadcast_to([P, GB, E]), start=False, stop=True,
                                 skip_group_check=True).then_inc(prep_full, 1)

            def body(g, par, is_first, is_last, pairs):
                for u in range(UPG):
                    if u < UPG - 2:
                        scores(g, par, u + 2)
                    elif not is_last:
                        scores(g + 1, 1 - par, u + 2 - UPG)
                    scores_T(g, par, u)
                    if u == 4 and not is_last:
                        prep_k(g)
                    if not (is_first and u == 0):
                        values(g, u - 1)
                    if u == 1:
                        project_v(g, 3)
                        if not is_first:
                            o_T(g, 3)
                    if not is_last:
                        if u == 2:
                            prep_c(g)
                        if u == 3:
                            prep_x(g)
                        if u in (7, 8, 12):
                            project_v(g, (7, 8, 12).index(u))
                    if not is_first:
                        if u == 2:
                            a_T(g, 3)
                        if u == 3:
                            y_out(g, 3)
                        if u == 9:
                            x2_T(g, 1 - par)
                        if u == 10:
                            logits(g)
                        if u == 13:
                            rank(g)
                    if u in (5, 9, 13):
                        o_T(g, (u - 5) // 4)
                    if u == 5 and not is_last:
                        prep_q(g)
                    if u in (6, 10, 14):
                        a_T(g, (u - 6) // 4)
                    if u in (7, 11, 15):
                        y_out(g, (u - 7) // 4)

            pe.wait_ge(ident_here, 16)
            prep_c(-1)
            pe.wait_ge(wk_here, 32)
            prep_k(-1)
            prep_x(-1)
            pe.wait_ge(wq_here, 32)
            prep_q(-1)
            pe.wait_ge(w_in, 16 * 4)
            project_v(-1, 0)
            project_v(-1, 1)
            project_v(-1, 2)
            pe.wait_ge(setup, 2)
            scores(0, 0, 0)
            scores(0, 0, 1)
            pe.wait_ge(w_in2, 16 * 5)
            bodies(pe, body)
            values(NG, -1)
            o_T(NG, 3)
            a_T(NG, 3)
            y_out(NG, 3)
            x2_T(NG, 1)
            logits(NG)
            rank(NG)
            wait(pe, tail_free, 12 * NG)
            pe.wait_ge(route_c, ROUTE * NG)
            nc.tensor.matmul(tail[:, 0:E], ones[:, :], mcarry[:, :], start=True, stop=True).then_inc(cnt_full, 1)
            pe.wait_ge(table_c, TABLE)
            pe.wait_ge(ffn_in, 16 * 2)

            def x_T(i, r, turn):
                pe.wait_ge(x_tile[r], 16 * (turn + 1))
                wait(pe, xl_done, i)
                for h in range(2):
                    last = nc.tensor.transpose(xT_bank[:, h * P:(h + 1) * P], xt[:, r, h, 0:D], ident[:, :])
                last.then_inc(xT_full, 1)

            def up(i, r, e):
                pe.wait_ge(xl_done, i + 1)
                wait(pe, h_done, MC * (i - 2))
                for c in range(MC):
                    o = h_bank[r][c // 2][:, (c % 2) * TR:(c % 2) * TR + TR]
                    cols = slice(c * P, (c + 1) * P)
                    nc.tensor.matmul(o, w1_hi[:, e, cols], xh[:, r, :], start=True, stop=False)
                    nc.tensor.matmul(o, w1_hi[:, e, cols], xl[:, r, :], start=False, stop=False)
                    nc.tensor.matmul(o, w1_lo[:, e, cols], xh[:, r, :], start=False, stop=True).then_inc(h_full, 1)

            def down(i, r, e):
                wait(pe, yb_done, i)
                pe.wait_ge(hlo_done, i + 1)
                for h in range(2):
                    for c in range(MC):
                        o, rows, cols = y_bank[:, h * D:(h + 1) * D], slice(c * TR + h * P, c * TR + (h + 1) * P), slice(c * D, (c + 1) * D)
                        nc.tensor.matmul(o, h_hi[:, r, rows], w2_hi[:, e, cols], start=(c == 0), stop=False, skip_group_check=True)
                        nc.tensor.matmul(o, h_hi[:, r, rows], w2_lo[:, e, cols], start=False, stop=False, skip_group_check=True)
                        last = nc.tensor.matmul(o, h_lo[:, r, rows], w2_hi[:, e, cols], start=False, stop=(c == MC - 1), skip_group_check=True)
                last.then_inc(y_full, 1)

            for r in range(PING):
                x_T(r, r, 0)
            e = load_row(pe, tile_e, 0, 0, 2, E - 1)
            up(0, 0, e[0])
            up(1, 1, e[1])

            def tiles(n, is_last):
                e = load_row(pe, tile_e, n, 0, PING if is_last else AHEAD, E - 1)
                for r in range(PING):
                    i = n * PING + r
                    if not is_last:
                        x_T(i + 3, r, n + 1)
                    if not is_last or r < PING - 2:
                        up(i + 2, (r + 2) % PING, e[r + 2])
                    down(i, r, e[r])

            tiles(0, False)
            with pe.Fori(1, TURNS - 1) as n:
                tiles(n, False)
            tiles(TURNS - 1, True)

        @block.scalar
        def _(act):
            def col(t, i):
                return t[:, i:i + 1] if isinstance(i, int) else t[:, bass.ds(i, 1)]

            copy = lambda out_, in_: nc.scalar.activation(out_, in_, ACT.Copy)

            def exp(g, u):
                act.wait_ge(scoredT, UPG * g + u + 1)
                wait(act, pv_done, UPG * g + u - 3)
                nc.scalar.activation(probs[:, u % 4].rearrange("p j q -> p (j q)"), t_bank[u % 2][:, :], ACT.Exp,
                                     scale=DK ** -0.5).then_inc(exped, 1)

            def prep_copy(g, what, dst):
                act.wait_ge(prep_full, prep_use(g, what) + 1)
                copy(dst, bank_of(g, what)[:, :]).then_inc(xc_done, 1)

            def split_hi(g, t, n):
                act.wait_ge(prep_full, prep_use(g, t.upper()) + 1)
                wait(act, bounced[t], 16 * 4 * (g + 1))
                nc.scalar.activation(parts[t][:, 0, :], bank_of(g, t.upper())[:, :], ACT.Identity, bias=(bq_c if t == "q" else bk_c)[:, 0:1]).then_inc(hi_done, 1)

            def ln1(g, batches):
                act.wait_ge(ln1_rs, RSTEPS * (g + 2 if isinstance(g, int) and g < 1 else NG // 2 + 1))
                for b in batches:
                    last = nc.scalar.activation(xn[:, b, :], x_all[:, g * GB + GB + b, :], ACT.Identity, bias=col(nb1, g * GB + GB + b), scale=col(rs1, g * GB + GB + b))
                if b == GB - 1:
                    last.then_inc(ln1_done, 1)

            def o_copy(g, b):
                done = NS * (GB * g + (b + 1 if b < 3 else 0))
                act.wait_ge(pv_done, done)
                if b < 3 and isinstance(g, int) and g == 0 and b == 0:
                    pass
                else:
                    act.wait_ge(tail_full, (tail_use(g - 1, "OT2") if b == 3 else tail_use(g, "OT3" if b == 0 else f"OT{b - 1}")) + 1)
                copy(o_sb[:, :], o_bank[b % 2][:, :]).then_inc(o_out, 1)

            def a_copy(g, b):
                act.wait_ge(tail_full, tail_use(g, f"aT{b}") + 1)
                copy(aT[:, :], tail[:, 0:P]).then_inc(tail_free, 1)

            def ln2(g, par, pairs, batches):
                act.wait_ge(ln2_rs, RSTEPS * g)
                act.wait_ge(scattered[par], GB * TOPK * 16 * pairs + 16)
                for b in batches:
                    last = nc.scalar.activation(pay[:, par, b, :, 0:D], x_all[:, g * GB - GB + b, :].unsqueeze(1).broadcast_to([P, TOPK, D]), ACT.Identity,
                                                bias=nb2[:, b:b + 1], scale=rs2[:, b:b + 1])
                if b == GB - 1:
                    last.then_inc(ln2_done, 1)

            def x2_copy(g):
                act.wait_ge(prep_full, prep_use(g, "x2T") + 1)
                copy(x2T[:, :], prep[:, :]).then_inc(x2T_done, 1)

            def w1_split(g):
                act.wait_ge(w1_ready, 16 * (g + 1))
                nc.scalar.activation(w1_hi[:, g, :], w1_stage[:, :], ACT.Copy, scale=W_SCALE).then_inc(w1hi_done, 1)

            def w2_split(g):
                act.wait_ge(w2_ready, 16 * (g + 1))
                nc.scalar.activation(w2_hi[:, g, :], w2_stage[:, :], ACT.Copy, scale=W_SCALE).then_inc(w2hi_done, 1)

            def body(g, par, is_first, is_last, pairs):
                for u in range(UPG):
                    exp(g, u)
                    if not is_last:
                        if u == 2:
                            prep_copy(g, "cT", cT[:, :])
                        if u < 3:
                            ln1(g, ((0,), (1, 2), (3,))[u])
                        if u == 3:
                            prep_copy(g, "xT", xnT[:, :])
                        if u in (4, 5):
                            split_hi(g, "kq"[u - 4], u - 4)
                    if not is_first:
                        if u == 0:
                            o_copy(g, 3)
                        if u == 2:
                            a_copy(g, 3)
                        if u in (7, 8):
                            ln2(g, 1 - par, pairs, (0, 1) if u == 7 else (2, 3))
                        if u == 9:
                            x2_copy(g)
                    if u in (4, 8, 12):
                        o_copy(g, u // 4 - 1)
                    if u in (6, 10, 14):
                        a_copy(g, (u - 6) // 4)
                    if u == 13:
                        w1_split(g)
                    if u == 15:
                        w2_split(g)

            prep_copy(-1, "cT", cT[:, :])
            act.wait_ge(wk_here, 32)
            split_hi(-1, "k", 0)
            ln1(-1, range(GB))
            prep_copy(-1, "xT", xnT[:, :])
            act.wait_ge(wq_here, 32)
            split_hi(-1, "q", 1)
            act.wait_ge(w_in, 16 * 4)
            nc.scalar.activation(gate[:, :], gate_in[:, :], ACT.Tanh).then_inc(gates_done, 1)
            bodies(act, body)
            o_copy(NG, 3)
            a_copy(NG, 3)
            ln2(NG, 1, NG // 2 - 1, range(GB))
            x2_copy(NG)
            act.wait_ge(table_c, T_FILL)
            for e in range(1, E, 2):
                at = act.value_load(fill_i[0:1, e:e + 1], min_val=e * RS, max_val=e * RS + NTOK)
                act.dma_start(rows_dram[bass.ds(at, TR), :].rearrange("(p h) c -> p h c", h=2), pad[:, :, :]).then_inc(filled, 16)
            act.wait_ge(dz_done, 1)
            nc.scalar.activation(ez[:, :, :], dz[:, :, :], ACT.Exp).then_inc(ez_done, 1)
            nc.scalar.activation(gelu_warm[:, :], gate[:, 0:1], ACT.Gelu).then_inc(warm, 1)
            act.wait_ge(table_c, TABLE)
            act.wait_ge(ffn_in, 16 * 2)

            def x_hi(i, r):
                act.wait_ge(xT_full, i + 1)
                copy(xh[:, r, :], xT_bank[:, 0:TR]).then_inc(xh_done, 1)

            def gelu(i, r, e):
                wait(act, hlo_done, i - PING + 1)
                for c in range(MC):
                    act.wait_ge(h_full, MC * i + c + 1 if c % 2 else MC * i + c + 2)
                    nc.scalar.activation(hT[:, r, c * TR:(c + 1) * TR], h_bank[r][c // 2][:, (c % 2) * TR:(c % 2) * TR + TR], ACT.Gelu,
                                         bias=b1_c[:, e, c:c + 1], scale=1.0 / W_SCALE).then_inc(h_done, 1)

            def h_high(i, r):
                act.wait_ge(h_done, MC * i + MC)
                wait(act, y_full, i - PING + 1)
                copy(h_hi[:, r, :], hT[:, r, :]).then_inc(hhi_done, 1)

            for r in range(PING):
                x_hi(r, r)
            gelu(0, 0, load_row(act, tile_e, 0, 0, 1, E - 1)[0])
            h_high(0, 0)

            def tiles(n, is_last):
                e = load_row(act, tile_e, n, 0, PING if is_last else PING + 1, E - 1)
                for r in range(PING):
                    i = n * PING + r
                    if not is_last or r < PING - 1:
                        gelu(i + 1, (r + 1) % PING, e[r + 1])
                    if not is_last:
                        x_hi(i + 3, r)
                    if not is_last or r < PING - 1:
                        h_high(i + 1, (r + 1) % PING)

            tiles(0, False)
            with act.Fori(1, TURNS - 1) as n:
                tiles(n, False)
            tiles(TURNS - 1, True)

            ov = out.rearrange("b p d -> p b d")
            for g in range(NG):
                act.wait_ge(sum_c, 2 * g + 2)
                act.dma_start(ov[:, g * GB:(g + 1) * GB, :], x_all[:, g * GB:(g + 1) * GB, :]).then_inc(out_done, 16)

        @block.vector
        def _(dve):
            vec = nc.vector

            def maxima(g, u):
                dve.wait_ge(scored, UPG * g + u + 1)
                vec.reduce_max(maxes[:, u, :], s_bank[u % 2][:, :].rearrange("p (j k) -> p j k", j=NJ), AX_X).then_inc(maxed, 1)

            def v_out(g, b):
                dve.wait_ge(prep_full, prep_use(g, f"V{b}") + 1)
                vec.tensor_tensor(v_aug[:, b, :, 0:DK], bank_of(g, f"V{b}")[:, 0:D].rearrange("p (h d) -> p h d", h=NH),
                                  bv_b[:, :].rearrange("p (h d) -> p h d", h=NH), ALU.add).then_inc(v_done, 1)

            def split_lo(g, t, n):
                dve.wait_ge(hi_done, 2 * g + 2 + n + 1)
                wait(dve, bounced[t], 16 * 4 * (g + 1))
                vec.scalar_tensor_tensor(parts[t][:, 1, :], bank_of(g, t.upper())[:, :], (bq_c if t == "q" else bk_c)[:, 0:1], parts[t][:, 0, :],
                                         ALU.add, ALU.subtract).then_inc(lo_done, 1)

            def normalise(g, b):
                at = (GB * g + b) if b < 3 else GB * g - 1
                dve.wait_ge(tail_full, tail_use(g, f"OT{b}") + 1)
                heads = tail[:, :].rearrange("p (s j w) -> p s j w", s=NS, j=NJ)
                vec.reciprocal(rl[:, :, :], heads[:, :, :, DK]).then_inc(norm_c, 1)
                dve.wait_ge(norm_c, at + 1)
                vec.tensor_tensor(a_sb[:, :].rearrange("p (j s d) -> p s j d", j=NJ, s=NS), heads[:, :, :, 0:DK],
                                  rl[:, :, :].unsqueeze(3).broadcast_to([P, NS, NJ, DK]), ALU.mult).then_inc(tail_free, 1)

            def residual(g, b):
                at = (GB * g + b) if b < 3 else GB * g - 1
                if b == 0:
                    dve.wait_ge(x_plus, g + 1)
                dve.wait_ge(tail_full, tail_use(g, f"y{b}") + 1)
                vec.scalar_tensor_tensor(x_all[:, at, :], tail[:, 0:D], gate[:, 0:1], x_all[:, at, :], ALU.mult, ALU.add).then_inc(tail_free, 1)

            def stats2(g, b):
                at = (GB * g + b) if b < 3 else GB * g - 1
                dve.wait_ge(tail_free, tail_use(g, f"y{b}") + 1)
                apart(dve)
                vec.bn_stats(st2[:, b, :], x_all[:, at, :]).then_inc(ln2_stats, 1)

            def aggregate2(g, b, par):
                at = (GB * g + b) if b < 3 else GB * g - 1
                dve.wait_ge(ln2_stats, 2 * at + 1)
                apart(dve)
                vec.bn_aggr(mv2[:, par, b, :], st2[:, b, :]).then_inc(ln2_stats, 1)

            def stats1(group):
                for b in range(group * GB, group * GB + GB):
                    last = vec.bn_stats(st1[:, b, :], x_all[:, b, :])
                last.then_inc(ln1_stats, 1)

            def aggregate1(group):
                dve.wait_ge(ln1_stats, 2 * group + 1)
                for b in range(group * GB, group * GB + GB):
                    last = vec.bn_aggr(mv1[:, b, :], st1[:, b, :])
                last.then_inc(ln1_stats, 1)

            def after(g, step):
                dve.wait_ge(route_c, ROUTE * (g - 1) + step)

            def route_logits(g):
                dve.wait_ge(prep_full, prep_use(g, "logits") + 1)
                vec.tensor_tensor(lg[:, :, :], prep[:, 0:GB * E].rearrange("p (b e) -> p b e", b=GB),
                                  br_b[:, :].unsqueeze(1).broadcast_to([P, GB, E]), ALU.add).then_inc(lg_done, 1)

            def route_max(g):
                dve.wait_ge(lg_done, 2 * g + 1)
                apart(dve)
                for b in range(GB):
                    last = vec.max(t8[:, b, :], lg[:, b, :])
                last.then_inc(route_c, 1)

            def route_index(g):
                after(g, R_MAX)
                apart(dve)
                for b in range(GB):
                    last = vec.max_index(ti[:, b, :], t8[:, b, :], lg[:, b, :])
                last.then_inc(route_c, 1)
                vec.tensor_copy(t8_all[:, bass.ds((g - 1) * GB, GB), :], t8[:, :, :]).then_inc(kept, 1)

            def route_masks(g):
                after(g, R_INDEX)
                for k in range(TOPK):
                    last = vec.tensor_tensor(mk[:, :, k, :], consts[:, C_IOTA:C_IOTA + E].unsqueeze(1).broadcast_to([P, GB, E]),
                                             ti[:, :, k:k + 1].broadcast_to([P, GB, E]), ALU.is_equal)
                last.then_inc(route_c, 1)

            def route_both(g):
                after(g, R_MASK)
                vec.tensor_tensor(mboth[:, :, :], mk[:, :, 0, :], mk[:, :, 1, :], ALU.add).then_inc(route_c, 1)

            def route_sum(g):
                after(g, R_BOTH)
                vec.reduce_sum(msum[:, :], mboth[:, :, :].rearrange("p b e -> p e b"), AX_X).then_inc(route_c, 1)

            def route_rank(g):
                dve.wait_ge(prep_full, prep_use(g, "rank") + 1)
                vec.tensor_tensor(rank_b[:, :, :], prep[:, 0:GB * E].rearrange("p (b e) -> p b e", b=GB),
                                  consts[:, C_BASE:C_BASE + E].unsqueeze(1).broadcast_to([P, GB, E]), ALU.add).then_inc(lg_done, 1)

            def route_select(g):
                dve.wait_ge(lg_done, 2 * g + 2)
                after(g, R_SUM)
                for k in range(TOPK):
                    last = vec.tensor_tensor(sel[:, :, k, :], mk[:, :, k, :], rank_b[:, :, :], ALU.mult)
                last.then_inc(route_c, 1)

            def route_slot(g):
                after(g, R_SEL)
                vec.reduce_sum(slot_f[:, :, :], sel[:, :, :, :], AX_X).then_inc(route_c, 1)

            def route_slot_i(g, par):
                after(g, R_SLOT)
                vec.tensor_copy(slot_i[:, par, :], slot_f[:, :, :].rearrange("p b k -> p (b k)")).then_inc(route_c, 1)
                vec.tensor_tensor(mcarry[:, :], mcarry[:, :], msum[:, :], ALU.add).then_inc(route_c, 1)

            def w1_low(g):
                dve.wait_ge(w1hi_done, g + 1)
                vec.scalar_tensor_tensor(w1_lo[:, g, :], w1_stage[:, :], W_SCALE, w1_hi[:, g, :], ALU.mult, ALU.subtract).then_inc(w1lo_done, 1)

            def w2_low(g):
                dve.wait_ge(w2hi_done, g + 1)
                vec.scalar_tensor_tensor(w2_lo[:, g, :], w2_stage[:, :], W_SCALE, w2_hi[:, g, :], ALU.mult, ALU.subtract).then_inc(w2lo_done, 1)

            def body(g, par, is_first, is_last, pairs):
                for u in range(UPG):
                    if u < UPG - 2:
                        maxima(g, u + 2)
                    elif not is_last:
                        maxima(g + 1, u + 2 - UPG)
                    if u == 1:
                        v_out(g, 3)
                    if not is_last:
                        if u == 4:
                            split_lo(g, "k", 0)
                        if u in (7, 8, 12):
                            v_out(g, (7, 8, 12).index(u))
                    if is_first and u >= 4:
                        if u == 4:
                            dve.wait_ge(x_rest, 16)
                        (aggregate1 if u % 2 else stats1)(u // 2)
                    if not is_first:
                        if u == 1:
                            normalise(g, 3)
                        if u == 3:
                            residual(g, 3)
                        if u == 4:
                            stats2(g, 3)
                        if u == 5:
                            aggregate2(g, 3, 1 - par)
                        if u == 10:
                            route_logits(g)
                        if u == 11:
                            route_max(g)
                    if u in (5, 9, 13):
                        normalise(g, (u - 5) // 4)
                    if u == 5 and not is_last:
                        split_lo(g, "q", 1)
                    if u in (7, 11, 15):
                        residual(g, (u - 7) // 4)
                    if not is_first:
                        if u == 11:
                            route_index(g)
                        if u == 12:
                            route_masks(g)
                    if u == 0 and not is_first:
                        w1_low(g - 1)
                    if u == 2 and not is_first:
                        w2_low(g - 1)
                    if not is_first:
                        if u == 12:
                            route_both(g)
                            route_sum(g)
                        if u == 13:
                            route_rank(g)
                        if u == 14:
                            route_select(g)
                            route_slot(g)
                            route_slot_i(g, 1 - par)
                    if u in (8, 12):
                        stats2(g, (u - 8) // 4)
                    if u in (9, 13):
                        aggregate2(g, (u - 9) // 4, par)
                stats2(g, 2)
                aggregate2(g, 2, par)

            vec.memset(diag["k"][:, 0].rearrange("p j s t -> p (j s t)").bitcast(U32), 0).then_inc(zeroed["k"][0], 1)
            dve.wait_ge(x_first, 16)
            stats1(0)
            aggregate1(0)
            vec.memset(ones[:, :], 1.0)
            vec.memset(mcarry[:, :], 0.0)
            vec.memset(ones8[:, :], 1.0).then_inc(setup, 1)
            dve.sem_inc(lg_done, 2)
            dve.wait_ge(ident_here, 16)
            vec.tensor_scalar(neg_ident[:, :], ident[:, :], -1.0, None, ALU.mult).then_inc(setup, 1)
            dve.wait_ge(wk_here, 32)
            split_lo(-1, "k", 0)
            dve.wait_ge(wq_here, 32)
            split_lo(-1, "q", 1)
            dve.wait_ge(w_in, 16 * 4)
            dve.wait_ge(v_zeroed, 2)
            for b in range(GB - 1):
                v_out(-1, b)
            dve.wait_ge(gates_done, 1)
            vec.tensor_scalar(gbo[:, :], bo_b[:, :], gate[:, 0:1], None, ALU.mult).then_inc(gbo_done, 1)
            dve.wait_ge(x_second, 16)
            stats1(1)
            aggregate1(1)
            dve.wait_ge(w_in2, 16 * 5)
            vec.tensor_copy(tri[:, :], tri32[:, :]).then_inc(tri_done, 1)
            maxima(0, 0)
            maxima(0, 1)
            bodies(dve, body)
            w1_low(NG - 1)
            w2_low(NG - 1)
            normalise(NG, 3)
            residual(NG, 3)
            stats2(NG, 3)
            aggregate2(NG, 3, 1)
            for piece in (route_logits, route_max, route_index, route_masks, route_both, route_sum, route_rank, route_select, route_slot):
                piece(NG)
            route_slot_i(NG, 1)

            c = Chain(dve, table_c, TABLE, 0)
            dve.wait_ge(cnt_full, 1)
            c.link(vec.tensor_copy(cnt[:, :], tail[:, 0:E]))
            c.link(vec.tensor_tensor(fill_f[:, :], cnt[:, :], consts[:, C_BASE:C_BASE + E], ALU.add))
            c.step(vec.tensor_copy(fill_i[:, :], fill_f[:, :]))
            c.link(vec.tensor_tensor(over[:, :, :], cnt[:, :].unsqueeze(2).broadcast_to([P, E, MAXT]),
                                     consts[:, C_STEP:C_STEP + MAXT].unsqueeze(1).broadcast_to([P, E, MAXT]), ALU.is_gt))
            c.link(vec.reduce_sum(ntile[:, :], over[:, :, :], AX_X))
            c.link(vec.tensor_tensor_scan(ntile_end[:, :], ones8[:, :], ntile[:, :], 0.0, ALU.mult, ALU.add))
            tiles_c = consts[:, C_TILE:C_TILE + TURNS * AHEAD]
            turns = lambda t: t.rearrange("p (n k) -> p n k", n=TURNS)
            c.link(vec.tensor_tensor(past[:, :, :], tiles_c.unsqueeze(2).broadcast_to([P, TURNS * AHEAD, E]),
                                     ntile_end[:, :].unsqueeze(1).broadcast_to([P, TURNS * AHEAD, E]), ALU.is_ge))
            c.step(vec.reduce_sum(te[:, :], past[:, :, :], AX_X))
            c.link(vec.tensor_tensor(pastn[:, :, :], past[:, :, :], ntile[:, :].unsqueeze(1).broadcast_to([P, TURNS * AHEAD, E]), ALU.mult))
            c.link(vec.reduce_sum(tprev[:, :], pastn[:, :, :], AX_X))
            c.link(vec.tensor_tensor(ta[:, :], tiles_c, tprev[:, :], ALU.subtract))
            c.link(vec.tensor_scalar(tb[:, :], te[:, :], float(RS), None, ALU.mult))
            c.link(vec.scalar_tensor_tensor(tr[:, :], ta[:, :], float(TR), tb[:, :], ALU.mult, ALU.add))
            c.step(vec.tensor_scalar(tile_row[:, :, 0:AHEAD], turns(tr[:, :]), float(E * RS), None, ALU.min))
            c.link(vec.tensor_scalar(tile_e[:, :, 0:AHEAD], turns(te[:, :]), float(E - 1), None, ALU.min))

            dve.wait_ge(kept, NG)
            vec.tensor_tensor(dz[:, :, :], t8_all[:, :, :], t8_all[:, :, 0:1].broadcast_to([P, NB, E]), ALU.subtract).then_inc(dz_done, 1)
            dve.wait_ge(ez_done, 1)
            c = Chain(dve, weight_c, WSTEPS, 0)
            c.link(vec.reduce_sum(z1[:, :], ez[:, :, :], AX_X))
            c.link(vec.reciprocal(z2[:, :], z1[:, :]))
            c.link(vec.tensor_tensor(pk[:, :, :], ez[:, :, 0:TOPK], z2[:, :].unsqueeze(2).broadcast_to([P, NB, TOPK]), ALU.mult))
            c.link(vec.reduce_sum(z3[:, :], pk[:, :, :], AX_X))
            c.link(vec.tensor_scalar(z4[:, :], z3[:, :], MOE_EPS, None, ALU.add))
            c.link(vec.reciprocal(z5[:, :], z4[:, :]))
            c.link(vec.tensor_tensor(wk2[:, :, :], pk[:, :, :], z5[:, :].unsqueeze(2).broadcast_to([P, NB, TOPK]), ALU.mult))
            c.link(vec.reduce_sum(z6[:, :], wk2[:, :, :], AX_X))
            c.link(vec.tensor_scalar(z7[:, :], z6[:, :], MOE_EPS, None, ALU.add))
            c.link(vec.reciprocal(z8[:, :], z7[:, :]))
            c.step(vec.scalar_tensor_tensor(weight[:, :, :], wk2[:, :, :], gate[:, 1:2], z8[:, :].unsqueeze(2).broadcast_to([P, NB, TOPK]),
                                            ALU.mult, ALU.mult))

            dve.wait_ge(ffn_in, 16 * 2)

            def x_lo(i, r):
                dve.wait_ge(xh_done, i + 1)
                vec.tensor_tensor(xl[:, r, :], xT_bank[:, 0:TR], xh[:, r, :], ALU.subtract).then_inc(xl_done, 1)

            def keep_rows(i, r):
                dve.wait_ge(xT_full, i + 1)
                wait(dve, dest_done, i - PING + 1)
                vec.tensor_copy(row_ids[:, r, :], xt[:, r, :, D]).then_inc(taken, 1)

            def y_end(i, r, turn, e):
                dve.wait_ge(y_full, i + 1)
                wait(dve, y_tile[r], 32 * turn)
                vec.scalar_tensor_tensor(yb[:, r], y_bank[:, 0:2 * D].rearrange("p (h d) -> p h d", h=2), 1.0 / W_SCALE,
                                         b2_b[:, e, :].unsqueeze(1).broadcast_to([P, 2, D]), ALU.mult, ALU.add).then_inc(yb_done, 1)
                dve.wait_ge(taken, i + 1)
                vec.tensor_copy(dest[:, r, :], row_ids[:, r, :]).then_inc(dest_done, 1)

            def h_low(i, r):
                dve.wait_ge(hhi_done, i + 1)
                wait(dve, y_full, i - PING + 1)
                vec.tensor_tensor(h_lo[:, r, :], hT[:, r, :], h_hi[:, r, :], ALU.subtract).then_inc(hlo_done, 1)

            for r in range(PING):
                x_lo(r, r)
                if r < PING - 1:
                    keep_rows(r, r)
            h_low(0, 0)

            def tiles(n, is_last):
                e = load_row(dve, tile_e, n, 0, PING, E - 1)
                for r in range(PING):
                    i = n * PING + r
                    if not is_last:
                        x_lo(i + 3, r)
                    if not is_last or r < PING - 2:
                        keep_rows(i + 2, (r + 2) % PING)
                    if not is_last or r < PING - 1:
                        h_low(i + 1, (r + 1) % PING)
                    y_end(i, r, n, e[r])

            tiles(0, False)
            with dve.Fori(1, TURNS - 1) as n:
                tiles(n, False)
            tiles(TURNS - 1, True)

            for g in range(NG):
                dve.wait_ge(y_ready[g], 16 * TOPK)
                if g == 0:
                    dve.wait_ge(weight_c, WSTEPS)
                for k in range(TOPK):
                    if k:
                        dve.wait_ge(sum_c, 2 * g + 1)
                    for b in range(GB):
                        at = g * GB + b
                        last = vec.scalar_tensor_tensor(x_all[:, at, :], y_in[:, g, k, b, :], weight[:, at, k:k + 1], x_all[:, at, :],
                                                        ALU.mult, ALU.add)
                    last.then_inc(sum_c, 1)

        @block.gpsimd
        def _(pool):
            gp = nc.gpsimd

            def rstd(sem_, n, rs, nb, mv, k):
                c = Chain(pool, sem_, RSTEPS, n)
                apart(pool)
                c.link(gp.tensor_scalar(rs, mv[:, :, 1], LN_EPS, 1.0, ALU.add, ALU.mult))
                c.link(gp.tensor_tensor(rs, rs, neg_half[:, 0:k], ALU.pow))
                apart(pool)
                c.link(gp.tensor_scalar(nb, mv[:, :, 0], -1.0, 0.0, ALU.mult, ALU.add))
                c.step(gp.tensor_tensor(nb, nb, rs, ALU.mult))

            def rstd1(n, first, end):
                pool.wait_ge(ln1_stats, 2 * end)
                b = slice(first * GB, end * GB)
                rstd(ln1_rs, n, rs1[:, b], nb1[:, b], mv1[:, b], (end - first) * GB)

            def rstd2(g, par):
                pool.wait_ge(ln2_stats, 2 * GB * g)
                rstd(ln2_rs, g - 1, rs2[:, :], nb2[:, :], mv2[:, par], GB)

            def add_bias(g):
                pool.wait_ge(ln1_done, g + 2)
                apart(pool)
                x4 = x_all[:, bass.ds(g * GB + GB, GB), :]
                gp.tensor_tensor(x4, x4, gbo[:, :].unsqueeze(1).broadcast_to([P, GB, D]), ALU.add).then_inc(x_plus, 1)

            def scatter(g, par, batches=range(GB)):
                if batches[0] == 0:
                    fill_ids(g, par)
                for b in batches:
                    for k in range(TOPK):
                        gp.indirect_dma_start(out=rows_dram, out_offset=bass.IndirectOffsetOnAxis(ap=slot_i[:, par, b * TOPK + k:b * TOPK + k + 1], axis=0),
                                              in_=pay[:, par, b, k, :], in_offset=None).then_inc(scattered[par], 16)

            def fill_ids(g, par):
                pool.wait_ge(ln2_done, g)
                apart(pool)
                ids = consts[:, bass.ds((g - 1) * (GB * TOPK) + C_ID, GB * TOPK)]
                gp.tensor_copy(pay[:, par, :, :, D],
                               ids.rearrange("p (b k) -> p b k", b=GB)).then_inc(ids_done, 1)
                pool.wait_ge(ids_done, g)
                pool.wait_ge(route_c, ROUTE * g)
                apart(pool)

            def body(g, par, is_first, is_last, pairs):
                if is_first:
                    for n in range(1, NG // 2):
                        rstd1(n + 1, 2 * n, 2 * n + 2)
                if not is_first:
                    rstd2(g, 1 - par)
                if not is_last:
                    add_bias(g)
                if not is_first:
                    scatter(g, 1 - par, range(GB // 2 if is_last else GB))

            def zero(t, par):
                gp.memset(diag[t][:, par].rearrange("p j s t -> p (j s t)").bitcast(U32), 0).then_inc(zeroed[t][par], 1)

            gp.memset(neg_half[:, :], -0.5).then_inc(half_done, 1)
            pool.wait_ge(half_done, 1)
            rstd1(0, 0, 1)
            zero("q", 0)
            gp.memset(v_aug[:, :, :, :], 0.0).then_inc(v_zeroed, 1)
            pool.wait_ge(v_zeroed, 1)
            gp.memset(v_aug[:, :, :, DK], 1.0).then_inc(v_zeroed, 1)
            rstd1(1, 1, 2)
            for t in "kq":
                zero(t, 1)
            pool.wait_ge(gbo_done, 1)
            add_bias(-1)
            gp.memset(pad[:, :, :], 0.0).then_inc(pad_done, 1)
            pool.wait_ge(pad_done, 1)
            gp.memset(pad[:, :, D], NOWHERE).then_inc(pad_done, 1)
            pool.wait_ge(pad_done, 2)
            for i in range(2):
                gp.dma_start(rows_dram[E * RS + i * P:E * RS + (i + 1) * P, :], pad[:, i, :]).then_inc(scattered[i], 16)
            bodies(pool, body)
            rstd2(NG, 1)
            scatter(NG - 1, 0, range(GB // 2, GB))
            scatter(NG, 1)

            def put(i, r):
                pool.wait_ge(yb_done, i + 1)
                pool.wait_ge(dest_done, i + 1)
                apart(pool)
                for h in range(2):
                    gp.indirect_dma_start(out=y_dram, out_offset=bass.IndirectOffsetOnAxis(ap=dest[:, r, h:h + 1], axis=0), in_=yb[:, r, h, :],
                                          in_offset=None, bounds_check=TOPK * NTOK - 1, oob_is_err=False).then_inc(y_tile[r], 16)

            with pool.Fori(0, TURNS) as n:
                for r in range(PING):
                    put(n * PING + r, r)


_INS = ['x', 'ctx_in', 'gates', 'wq', 'bq', 'wk', 'bk', 'wv', 'bv', 'wo', 'bo', 'wr', 'br', 'w1', 'b1', 'w2', 'b2', 'ident', 'tri', 'consts']


def kernel(**inputs):
    import concourse.bacc as _bacc
    from concourse.bass_utils import run_bass_kernel_spmd as _run

    a = {k: np.asarray(v) for k, v in inputs.items()}

    def by_block(w):
        return w.reshape(w.shape[:-1] + (NJ, NS, DK)).swapaxes(-1, -2).reshape(w.shape)

    consts = np.zeros(C_END, np.float32)
    consts[C_IOTA:C_IOTA + E] = np.arange(E)
    consts[C_BASE:C_BASE + E] = np.arange(E) * RS
    consts[C_TILE:C_TILE + TURNS * AHEAD] = np.minimum(np.arange(TURNS)[:, None] * PING + np.arange(AHEAD), NT - 1).reshape(-1)
    consts[C_STEP:C_STEP + MAXT] = np.arange(MAXT) * TR
    consts = np.tile(consts, (P, 1))
    token = np.arange(NB)[None, :, None] * P + np.arange(P)[:, None, None]
    consts[:, C_ID:] = (token + np.arange(TOPK)[None, None, :] * NTOK).reshape(P, NB * TOPK)
    host = {
        'x': a['x'], 'ctx_in': a['ctx_1024'], 'gates': np.concatenate([a['g_xattn'], a['g_ffn']]),
        'wq': by_block(a['L0_xattn_W_q'].T), 'bq': by_block(a['L0_xattn_b_q'])[:, None],
        'wk': by_block(a['L0_xattn_W_k'].T), 'bk': by_block(a['L0_xattn_b_k'])[:, None],
        'wv': a['L0_xattn_W_v'].T, 'bv': a['L0_xattn_b_v'], 'wo': a['L0_xattn_W_o'].T, 'bo': a['L0_xattn_b_o'],
        'wr': a['L0_ffn_Wr'], 'br': a['L0_ffn_br'], 'w1': a['L0_ffn_W1'],
        'b1': a['L0_ffn_b1'].reshape(E * MC, P).T,
        'w2': a['L0_ffn_W2'].reshape(E, MC, P, D).transpose(0, 2, 1, 3).reshape(E, P, MC * D), 'b2': a['L0_ffn_b2'],
        'ident': np.eye(P, dtype=np.float32), 'tri': np.triu(np.ones((P, P), np.float32), 1), 'consts': consts,
    }
    nc = _bacc.Bacc("TRN2", target_bir_lowering=False, num_devices=1)
    arrays, args = {}, []
    for name in _INS:
        v = np.ascontiguousarray(host[name])
        arrays["in_" + name] = v
        args.append(nc.dram_tensor("in_" + name, v.shape, mybir.dt.from_np(v.dtype), kind="ExternalInput").ap())
    args.append(nc.dram_tensor("out", (NB, P, D), F32, kind="ExternalOutput").ap())
    moe_attention(nc, *args)
    r = _run(nc, [arrays], core_ids=[0])
    return r.results[0]["out"]
```

```python
from contextlib import ExitStack

import numpy as np

import concourse.bass as bass
from concourse import mybir

ALU = mybir.AluOpType
ACT = mybir.ActivationFunctionType
AX_X = mybir.AxisListType.X
F32 = mybir.dt.float32
F16 = mybir.dt.float16
BF16 = mybir.dt.bfloat16
I32 = mybir.dt.int32
U32 = mybir.dt.uint32

P = 128
NB = 32
D = 128
NH, DK = 16, 8
NJ, NS = 4, 4
GB = 4
NG = NB // GB
GT = GB * P
UPG = GB * NS
E, M, TOPK = 8, 512, 2
MC = M // P
NTOK = NB * P
TR = 256
NT = (TOPK * NTOK + E * (TR - 1)) // TR
RS = NTOK + TR
ROWS = E * RS + TR
PW = D + 1
MAXT = NTOK // TR
LN_EPS, MOE_EPS = 1e-5, 1e-9
W_SCALE = 64.0
NOWHERE = float(4 * NTOK)
PING = 3
TURN = 2 * PING
TURNS = NT // TURN
AHEAD = TURN + 2
BITS = 3
assert NT == TURNS * TURN + PING and 1 << BITS == E

C_IOTA, C_BASE, C_TILE, C_STEP, C_ID = 0, E, 2 * E, 2 * E + (TURNS + 1) * AHEAD, 2 * E + (TURNS + 1) * AHEAD + MAXT
C_DIGIT = C_ID + NB * TOPK
C_END = C_DIGIT + AHEAD


def wait(eng, sem, value):
    if isinstance(value, int) and value <= 0:
        return
    eng.wait_ge(sem, value)


class Chain:

    def __init__(self, eng, sem, per, n):
        self.eng, self.sem, self.per, self.n, self.count = eng, sem, per, n, 0

    def step(self, ins):
        self.count += 1
        assert self.count <= self.per
        ins.then_inc(self.sem, 1)

    def settle(self):
        self.eng.wait_ge(self.sem, self.n * self.per + self.count)

    def link(self, ins):
        self.step(ins)
        self.settle()


def moe_attention(nc, x, ctx_in, gates, wq, bq, wk, bk, wv, bv, wo, bo, wr, br, w1, b1, w2, b2, ident_in, tri_in, consts_in, out):
    bounce = {t: nc.dram_tensor(f"bounce_{t}", (NJ, 4, DK, NS, GT), F16, kind="Internal").ap() for t in "qk"}
    rows_dram = nc.dram_tensor("rows_dram", (ROWS, PW), F32, kind="Internal").ap()
    y_dram = nc.dram_tensor("y_dram", (TOPK * NTOK, D), F32, kind="Internal").ap()

    with ExitStack() as stack:
        def sb(name, shape, dt=F32):
            return stack.enter_context(nc.sbuf_tensor(name, shape, dt))

        def psum(name, shape):
            return stack.enter_context(nc.psum_tensor(name, shape, F32))

        def sem(name):
            return stack.enter_context(nc.semaphore(name))

        ident = sb("ident", [P, P])
        neg_ident = sb("neg_ident", [P, P], BF16)
        tri32 = sb("tri32", [P, P])
        tri = sb("tri", [P, P], BF16)
        ones = sb("ones", [P, P], BF16)
        consts = sb("consts", [P, C_END])
        gate_in = sb("gate_in", [P, 2])
        gate = sb("gate", [P, 2])
        neg_half = sb("neg_half", [P, NB])
        wqT, wkT, wvT, woT = (sb(n, [P, D]) for n in ("wqT", "wkT", "wvT", "woT"))
        bq_c, bk_c = sb("bq_c", [P, 1]), sb("bk_c", [P, 1])
        bv_b, bo_b, gbo = sb("bv_b", [P, D]), sb("bo_b", [P, D]), sb("gbo", [P, D])
        wr_sb, br_b = sb("wr_sb", [P, E]), sb("br_b", [P, E])
        w1_stage = sb("w1_stage", [P, M])
        w1_hi, w1_lo = sb("w1_hi", [P, E, M], F16), sb("w1_lo", [P, E, M], F16)
        b1_c = sb("b1_c", [P, E, MC])
        w2_stage = sb("w2_stage", [P, MC * D])
        w2_hi, w2_lo = sb("w2_hi", [P, E, MC * D], F16), sb("w2_lo", [P, E, MC * D], F16)
        b2_b = sb("b2_b", [P, E, D])
        x_all = sb("x_all", [P, NB, D])
        c_in = sb("c_in", [P, GB, D])
        xn = sb("xn", [P, GB, D])
        st1, mv1, rs1, nb1 = sb("st1", [P, NB, 6]), sb("mv1", [P, NB, 2]), sb("rs1", [P, NB]), sb("nb1", [P, NB])
        st2, mv2, rs2, nb2 = sb("st2", [P, GB, 6]), sb("mv2", [P, 2, GB, 2]), sb("rs2", [P, GB]), sb("nb2", [P, GB])
        xnT, cT = sb("xnT", [P, GT]), sb("cT", [P, GT])
        parts = {t: sb(f"parts_{t}", [P, 2, GT], F16) for t in "qk"}
        plain = {t: sb(f"plain_{t}", [P, 2, NS, GT], F16) for t in "qk"}
        diag = {t: sb(f"diag_{t}", [P, 2, NJ, NS, GT], F16) for t in "qk"}
        v_aug = sb("v_aug", [P, GB, NH, 32])
        maxes = sb("maxes", [P, UPG, NJ], BF16)
        probs = sb("probs", [P, 4, NJ, P])
        o_sb = sb("o_sb", [P, NS * P])
        rl = sb("rl", [P, NS, NJ])
        a_sb, aT = sb("a_sb", [P, D]), sb("aT", [P, P])
        pay = sb("pay", [P, 2, GB, TOPK, PW])
        x2T = sb("x2T", [P, GT])
        lg, t8 = sb("lg", [P, GB, E]), sb("t8", [P, GB, E])
        ti = sb("ti", [P, GB, E], U32)
        mk, mboth = sb("mk", [P, GB, TOPK, E]), sb("mboth", [P, GB, E], BF16)
        mcarry, msum = sb("mcarry", [P, E], BF16), sb("msum", [P, E])
        t8_all, dz, ez = (sb(n, [P, NB, E]) for n in ("t8_all", "dz", "ez"))
        z1, z2, z3, z4, z5, z6, z7, z8 = (sb(f"z{i}", [P, NB]) for i in range(8))
        pk, wk2, weight = (sb(n, [P, NB, TOPK]) for n in ("pk", "wk2", "weight"))
        rank_b, sel, slot_f = sb("rank_b", [P, GB, E]), sb("sel", [P, GB, TOPK, E]), sb("slot_f", [P, GB, TOPK])
        slot_i = sb("slot_i", [P, 2, GB * TOPK], I32)
        cnt, fill_f, fill_i = sb("cnt", [P, E]), sb("fill_f", [P, E]), sb("fill_i", [P, E], I32)
        over, ntile, ntile_end = sb("over", [P, E, MAXT]), sb("ntile", [P, E]), sb("ntile_end", [P, E])
        past, pastn = sb("past", [P, (TURNS + 1) * AHEAD, E]), sb("pastn", [P, (TURNS + 1) * AHEAD, E])
        te, tprev, ta, tb, tr = (sb(n, [P, (TURNS + 1) * AHEAD]) for n in ("te", "tprev", "ta", "tb", "tr"))
        tile_row = sb("tile_row", [P, TURNS + 1, AHEAD], I32)
        digits = sb("digits", [P, TURNS + 1, AHEAD])
        packed_f, packed = sb("packed_f", [P, TURNS + 1]), sb("packed", [P, TURNS + 1], I32)
        pad = sb("pad", [P, 2, PW])
        gelu_warm = sb("gelu_warm", [P, 1])
        ones8 = sb("ones8", [P, E])
        xt = sb("xt", [P, PING, 2, PW])
        xh, xl = sb("xh", [P, PING, TR], F16), sb("xl", [P, PING, TR], F16)
        room_h = diag["k"][:, :, :, :, :].rearrange("p a j s t -> p (a j s t)")
        n_h = PING * MC * TR
        hT = room_h[:, 0:2 * n_h].bitcast(F32).rearrange("p (r m) -> p r m", r=PING)
        h_hi = room_h[:, 2 * n_h:3 * n_h].rearrange("p (r m) -> p r m", r=PING)
        h_lo = room_h[:, 3 * n_h:4 * n_h].rearrange("p (r m) -> p r m", r=PING)
        yb = plain["k"][:, :, :, :].rearrange("p a s t -> p (a s t)").bitcast(F32)[:, 0:PING * 2 * D].rearrange("p (r h d) -> p r h d", r=PING, h=2)
        row_ids, dest = sb("row_ids", [P, PING, 2]), sb("dest", [P, PING, 2], I32)
        y_in = diag["q"][:, :, :, :, :].rearrange("p a j s t -> p (a j s t)").bitcast(F32).rearrange("p (r k b d) -> p r k b d", r=NG, k=TOPK, b=GB)

        s_bank = [psum(f"s_bank{i}", [P, 512]) for i in range(2)]
        t_bank = [psum(f"t_bank{i}", [P, 512]) for i in range(2)]
        o_bank = [psum(f"o_bank{i}", [P, 512]) for i in range(2)]
        prep = psum("prep", [P, 512])
        tail = psum("tail", [P, 512])
        h_bank = [[s_bank[0], s_bank[1]], [t_bank[0], t_bank[1]], [o_bank[0], o_bank[1]]]
        xT_bank, y_bank = prep, tail

        x_first, x_second, x_rest, ident_here, wk_here, wq_here, w_in, w_in2 = (sem(n) for n in ("x_first", "x_second", "x_rest", "ident_here", "wk_here", "wq_here", "w_in", "w_in2"))
        c_ready, w1_ready, ffn_in = sem("c_ready"), sem("w1_ready"), sem("ffn_in")
        bounced = {t: sem(f"bounced_{t}") for t in "qk"}
        spread = {t: sem(f"spread_{t}") for t in "qk"}
        scattered, filled = [sem(f"scattered{i}") for i in range(2)], sem("filled")
        setup, gates_done, zeroed = sem("setup"), sem("gates_done"), {t: [sem(f"zeroed_{t}{i}") for i in range(2)] for t in "qk"}
        pad_done, v_zeroed = sem("pad_done"), sem("v_zeroed")
        gbo_done, half_done = sem("gbo_done"), sem("half_done")
        prep_full, v_done, xc_done = sem("prep_full"), sem("v_done"), sem("xc_done")
        tail_full, tail_free = sem("tail_full"), sem("tail_free")
        scored, maxed, scoredT, exped, pv_done, o_out = (sem(n) for n in ("scored", "maxed", "scoredT", "exped", "pv_done", "o_out"))
        ln1_stats, ln1_mean, ln1_rs, ln1_done, x_plus = (sem(n) for n in ("ln1_stats", "ln1_mean", "ln1_rs", "ln1_done", "x_plus"))
        ln2_stats, ln2_rs, ln2_done = (sem(n) for n in ("ln2_stats", "ln2_rs", "ln2_done"))
        hi_done, lo_done = sem("hi_done"), sem("lo_done")
        norm_c, x2T_done, lg_done, route_c, ids_done = (sem(n) for n in ("norm_c", "x2T_done", "lg_done", "route_c", "ids_done"))
        dz_done, ez_done, weight_c, kept, warm = (sem(n) for n in ("dz_done", "ez_done", "weight_c", "kept", "warm"))
        w1hi_done, w1lo_done = sem("w1hi_done"), sem("w1lo_done")
        w2_ready, w2hi_done, w2lo_done = sem("w2_ready"), sem("w2hi_done"), sem("w2lo_done")
        cnt_full, table_c = sem("cnt_full"), sem("table_c")
        taken = sem("taken")
        x_tile = [sem(f"x_tile{i}") for i in range(PING)]
        y_tile = [sem(f"y_tile{i}") for i in range(PING)]
        xT_full, xh_done, xl_done = sem("xT_full"), sem("xh_done"), sem("xl_done")
        h_full, h_done, hhi_done, hlo_done, y_full, yb_done, dest_done = (sem(n) for n in ("h_full", "h_done", "hhi_done", "hlo_done", "y_full", "yb_done", "dest_done"))
        y_ready = [sem(f"y_ready{i}") for i in range(NG)]
        first_added, weighted, summed = sem("first_added"), sem("weighted"), sem("summed")
        out_done = sem("out_done")
        RSTEPS, ROUTE, WSTEPS, TABLE = 4, 9, 11, 18
        T_FILL = 3
        R_MAX, R_INDEX, R_MASK, R_BOTH, R_SUM, R_SEL, R_SLOT, R_SLOT_I, R_CARRY = range(1, ROUTE + 1)

        PREP = ("V3", "cT", "xT", "K", "Q", "V0", "V1", "x2T", "logits", "V2", "rank")
        ROUTING = ("x2T", "logits", "rank")
        TAIL = tuple(w + str(b) for b in (3, 0, 1, 2) for w in ("OT", "aT", "y"))

        def prep_uses(g):
            if not isinstance(g, int) or 0 < g < NG - 1:
                return PREP
            if g == -1:
                return ("cT", "K", "xT", "Q", "V0", "V1", "V2")
            if g == 0:
                return tuple(w for w in PREP if w not in ROUTING)
            return ("V3",) + ROUTING if g == NG - 1 else ROUTING

        def prep_use(g, what):
            uses = prep_uses(g)
            if isinstance(g, int) and g < 1:
                return 7 * (g + 1) + uses.index(what)
            base = 15 + 11 * (NG - 2) + 4 if isinstance(g, int) and g == NG else g * 11 + 4
            return base + uses.index(what)

        def bank_of(g, what):
            own = {"cT": t_bank[1], "Q": s_bank[0], "K": s_bank[1], "V0": o_bank[0], "V1": o_bank[1]}
            return own.get(what, prep) if isinstance(g, int) and g < 0 else prep

        def prep_done(g, what):
            if what[0] == "V":
                return v_done, 4 * g + 4 + ("V3", "V0", "V1", "V2").index(what)
            if what in ("cT", "xT"):
                return xc_done, 2 * g + 3 + (what == "xT")
            if what in ("Q", "K"):
                return lo_done, 2 * g + 3 + (what == "Q")
            if what == "x2T":
                return x2T_done, g
            return lg_done, 2 * g + 1 + (what == "rank")

        def tail_use(g, what):
            return g * 12 - 3 + TAIL.index(what)

        def bodies(eng, body):
            body(0, 0, True, False, 0)
            with eng.Fori(0, (NG - 2) // 2) as n:
                body(n * 2 + 1, 1, False, False, n)
                body(n * 2 + 2, 0, False, False, n)
            body(NG - 1, 1, False, True, NG // 2 - 1)

        waited = {e: sem(f"waited_{n}") for n, e in (("sp", nc.sync.engine), ("act", nc.scalar.engine), ("dve", nc.vector.engine), ("pool", nc.gpsimd.engine))}

        def apart(eng):
            eng.sem_inc(waited[eng.engine], 1)

        def experts(eng, n):
            all_of_them = eng.value_load(packed[0:1, n:n + 1] if isinstance(n, int) else packed[0:1, bass.ds(n, 1)], min_val=0, max_val=E ** AHEAD - 1)
            return [(all_of_them >> (BITS * k)) & (E - 1) for k in range(AHEAD)]

        def x_bank(i):
            return h_bank[2][1] if isinstance(i, int) and i == 1 else xT_bank

        block = stack.enter_context(nc.Block())

        @block.sync
        def _(sp):
            xv = x.rearrange("b p d -> p b d")
            cv = ctx_in.rearrange("b p d -> p b d")
            sp.dma_start(x_all[:, 0:GB, :], xv[:, 0:GB, :]).then_inc(x_first, 16)
            sp.dma_start(c_in[:, :, :], cv[:, 0:GB, :]).then_inc(c_ready, 16)
            small = [(ident[:, :], ident_in, ident_here), (wkT[:, :], wk, wk_here), (bk_c[:, :], bk, wk_here), (wqT[:, :], wq, wq_here), (bq_c[:, :], bq, wq_here),
                     (wvT[:, :], wv, w_in), (bv_b[:, :], bv.partition_broadcast(P), w_in), (gate_in[:, :], gates.partition_broadcast(P), w_in),
                     (bo_b[:, :], bo.partition_broadcast(P), w_in)]
            for dst, src, here in small:
                sp.dma_start(dst, src).then_inc(here, 16)
            sp.dma_start(x_all[:, GB:2 * GB, :], xv[:, GB:2 * GB, :]).then_inc(x_second, 16)
            late = [(woT[:, :], wo), (wr_sb[:, :], wr), (br_b[:, :], br.partition_broadcast(P)), (tri32[:, :], tri_in),
                    (consts[:, :], consts_in)]
            for dst, src in late:
                sp.dma_start(dst, src).then_inc(w_in2, 16)

            def bounce_part(G, t, n):
                wait(sp, lo_done, 2 * G + n + 1)
                apart(sp)
                wait(sp, spread[t], 16 * 5 * G)
                for r in range(4):
                    part = r >> 1 if t == "q" else r & 1
                    sp.dma_start(bounce[t][:, r].rearrange("j i s t -> j (i s) t"), parts[t][:, part, :]).then_inc(bounced[t], 16)

            def spread_part(G, par, t):
                sp.wait_ge(bounced[t], 16 * 4 * (G + 1))
                apart(sp)
                wait(sp, scoredT, UPG * (G - 1))
                sp.wait_ge(zeroed[t][par], 1)
                sp.dma_start(plain[t][:, par], bounce[t].rearrange("j r i s t -> (j r i) s t")).then_inc(spread[t], 16)
                for j in range(NJ):
                    sp.dma_start(diag[t][32 * j:32 * j + 32, par, j], bounce[t][j].rearrange("r i s t -> (r i) s t")).then_inc(spread[t], 16)

            def body(g, par, is_first, is_last, pairs):
                if not is_last:
                    sp.wait_ge(*prep_done(g - 1, "cT"))
                    apart(sp)
                    sp.dma_start(c_in[:, :, :], cv[:, bass.ds(g * GB + GB, GB), :]).then_inc(c_ready, 16)
                wait(sp, w1lo_done, g)
                sp.dma_start(w1_stage[:, :], w1[g]).then_inc(w1_ready, 16)
                wait(sp, w2lo_done, g)
                sp.dma_start(w2_stage[:, :], w2[g]).then_inc(w2_ready, 16)
                if is_last:
                    for dst, src in [(b1_c[:, :, :].rearrange("p e c -> p (e c)"), b1), (b2_b[:, :, :], b2.partition_broadcast(P))]:
                        sp.dma_start(dst, src).then_inc(ffn_in, 16)
                    return
                if is_first:
                    sp.dma_start(x_all[:, 2 * GB:NB, :], xv[:, 2 * GB:NB, :]).then_inc(x_rest, 16)
                for n, t in enumerate("kq"):
                    bounce_part(g + 1, t, n)
                for t in "kq":
                    spread_part(g + 1, 1 - par, t)

            for n, t in enumerate("kq"):
                bounce_part(0, t, n)
            for t in "kq":
                spread_part(0, 0, t)
            bodies(sp, body)

            sp.wait_ge(table_c, T_FILL)
            for e in range(0, E, 2):
                at = sp.value_load(fill_i[0:1, e:e + 1], min_val=e * RS, max_val=e * RS + NTOK)
                sp.dma_start(rows_dram[bass.ds(at, TR), :].rearrange("(p h) c -> p h c", h=2), pad[:, :, :]).then_inc(filled, 16)
            sp.wait_ge(filled, 16 * E)
            sp.wait_ge(table_c, TABLE)
            for i in range(2):
                sp.wait_ge(scattered[i], 16 * GB * TOPK * NG // 2 + 16)

            def load_tile(i, r, n, k):
                row = tile_row[0:1, n, k:k + 1] if isinstance(n, int) else tile_row[0:1, bass.ds(n, 1), k:k + 1].rearrange("p n k -> p (n k)")
                at = sp.value_load(row, min_val=0, max_val=E * RS)
                wait(sp, taken, i - PING + 1)
                apart(sp)
                sp.dma_start(xt[:, r], rows_dram[bass.ds(at, TR), :].rearrange("(p h) c -> p h c", h=2)).then_inc(x_tile[r], 16)

            def load_tiles(n, size):
                for r in range(size):
                    load_tile(n * TURN + r, r % PING, n, r)

            load_tiles(0, TURN)
            with sp.Fori(1, TURNS) as n:
                load_tiles(n, TURN)
            load_tiles(TURNS, PING)

            for r in range(PING):
                sp.wait_ge(y_tile[r], 32 * (NT // PING))
            yv = y_dram.rearrange("(k b p) d -> k p b d", k=TOPK, p=P)
            for g in range(NG):
                for k in range(TOPK):
                    sp.dma_start(y_in[:, g, k], yv[k][:, g * GB:(g + 1) * GB, :]).then_inc(y_ready[g], 16)
            ov = out.rearrange("b p d -> p b d")
            for g in range(NG):
                sp.wait_ge(summed, g + 1)
                sp.dma_start(ov[:, g * GB:(g + 1) * GB, :], x_all[:, g * GB:(g + 1) * GB, :]).then_inc(out_done, 16)
            sp.wait_ge(out_done, 16 * NG)

        @block.tensor
        def _(pe):
            def prep_begin(g, what):
                uses = prep_uses(g)
                if isinstance(g, int) and g < 0:
                    if what == "V2":
                        pe.wait_ge(*prep_done(g, "xT"))
                elif what != uses[0]:
                    pe.wait_ge(*prep_done(g, uses[uses.index(what) - 1]))
                else:
                    if not (isinstance(g, int) and g == NG):
                        pe.wait_ge(*prep_done(g - 1, "V2"))
                    if not (isinstance(g, int) and g == 0):
                        pe.wait_ge(*prep_done(g - 1, "rank"))

            def tail_begin(g, what):
                wait(pe, tail_free, tail_use(g, what))

            def scores(g, par, u):
                if u == 0:
                    for t in "qk":
                        pe.wait_ge(spread[t], 16 * 5 * (g + 1))
                wait(pe, maxed, UPG * g + u - 1)
                b, s = u // NS, u % NS
                toks = slice(b * P, (b + 1) * P)
                nc.tensor.matmul(s_bank[u % 2][:, :], plain["q"][:, par, s, toks], diag["k"][:, par, :, s, toks],
                                 start=True, stop=True).then_inc(scored, 1)

            def scores_T(g, par, u):
                b, s = u // NS, u % NS
                toks = slice(b * P, (b + 1) * P)
                bank = t_bank[u % 2]
                wait(pe, exped, UPG * g + u - 1)
                nc.tensor.matmul(bank[:, :], plain["k"][:, par, s, toks], diag["q"][:, par, :, s, toks], start=True, stop=False,
                                 skip_group_check=True)
                pe.wait_ge(maxed, UPG * g + u + 1)
                for j in range(NJ):
                    last = nc.tensor.matmul(bank[:, j * P:(j + 1) * P], maxes[:, u, j:j + 1].broadcast_to([P, P]), neg_ident[:, :],
                                            start=False, stop=True, skip_group_check=True)
                last.then_inc(scoredT, 1)

            def values(g, u):
                if u < 0:
                    g, u = g - 1, UPG - 1
                b, s = u // NS, u % NS
                pe.wait_ge(exped, UPG * g + u + 1)
                if s == 0:
                    what = f"V{b}"
                    wait(pe, *prep_done(g if b == 3 else g - 1, what))
                    wait(pe, o_out, GB * g + b - 1)
                for j in range(NJ):
                    last = nc.tensor.matmul(o_bank[b % 2][32 * j:32 * j + 32, s * P:(s + 1) * P], v_aug[:, b, NJ * j + s, :],
                                            probs[:, u % 4, j, :], start=True, stop=True)
                last.then_inc(pv_done, 1)

            def project_v(g, b):
                prep_begin(g, f"V{b}")
                nc.tensor.matmul(bank_of(g, f"V{b}")[:, 0:D], cT[:, b * P:(b + 1) * P], wvT[:, :], start=True, stop=True).then_inc(prep_full, 1)

            def transpose4(bank, src):
                for b in range(GB):
                    last = nc.tensor.transpose(bank[:, b * P:(b + 1) * P], src(b), ident[:, :])
                return last

            def prep_x(g):
                prep_begin(g, "xT")
                pe.wait_ge(ln1_done, g + 2)
                transpose4(bank_of(g, "xT"), lambda b: xn[:, b, :]).then_inc(prep_full, 1)

            def prep_c(g):
                prep_begin(g, "cT")
                pe.wait_ge(c_ready, 16 * (g + 2))
                transpose4(bank_of(g, "cT"), lambda b: c_in[:, b, :]).then_inc(prep_full, 1)

            def prep_q(g):
                prep_begin(g, "Q")
                pe.wait_ge(*prep_done(g, "xT"))
                nc.tensor.matmul(bank_of(g, "Q")[:, :], wqT[:, :], xnT[:, :], start=True, stop=True).then_inc(prep_full, 1)

            def prep_k(g):
                prep_begin(g, "K")
                pe.wait_ge(*prep_done(g, "cT"))
                nc.tensor.matmul(bank_of(g, "K")[:, :], wkT[:, :], cT[:, :], start=True, stop=True).then_inc(prep_full, 1)

            def o_T(g, b):
                tail_begin(g, f"OT{b}")
                pe.wait_ge(o_out, GB * g + (b + 1 if b < 3 else 0))
                transpose4(tail, lambda s: o_sb[:, s * P:(s + 1) * P]).then_inc(tail_full, 1)

            def a_T(g, b):
                tail_begin(g, f"aT{b}")
                nc.tensor.transpose(tail[:, 0:P], a_sb[:, :], ident[:, :]).then_inc(tail_full, 1)

            def y_out(g, b):
                tail_begin(g, f"y{b}")
                nc.tensor.matmul(tail[:, 0:D], aT[:, :], woT[:, :], start=True, stop=True).then_inc(tail_full, 1)

            def x2_T(g, par):
                prep_begin(g, "x2T")
                pe.wait_ge(ln2_done, g)
                transpose4(prep, lambda b: pay[:, par, b, 0, 0:D]).then_inc(prep_full, 1)

            def logits(g):
                prep_begin(g, "logits")
                pe.wait_ge(x2T_done, g)
                for b in range(GB):
                    last = nc.tensor.matmul(prep[:, b * E:(b + 1) * E], x2T[:, b * P:(b + 1) * P], wr_sb[:, :], start=True, stop=True)
                last.then_inc(prep_full, 1)

            def rank(g):
                prep_begin(g, "rank")
                pe.wait_ge(route_c, ROUTE * (g - 1) + R_BOTH)
                out4 = prep[:, 0:GB * E].rearrange("p (b e) -> p b e", b=GB)
                nc.tensor.matmul(out4, tri[:, :], mboth[:, :, :], start=True, stop=False, skip_group_check=True)
                for k in range(1, GB):
                    nc.tensor.matmul(out4[:, k:GB, :], ones[:, :], mboth[:, 0:GB - k, :], start=False, stop=False, skip_group_check=True)
                nc.tensor.matmul(out4, ones[:, :], mcarry[:, :].unsqueeze(1).broadcast_to([P, GB, E]), start=False, stop=True,
                                 skip_group_check=True).then_inc(prep_full, 1)

            def body(g, par, is_first, is_last, pairs):
                for u in range(UPG):
                    if u < UPG - 2:
                        scores(g, par, u + 2)
                    elif not is_last:
                        scores(g + 1, 1 - par, u + 2 - UPG)
                    scores_T(g, par, u)
                    if u == 4 and not is_last:
                        prep_k(g)
                    if not (is_first and u == 0):
                        values(g, u - 1)
                    if u == 1:
                        project_v(g, 3)
                        if not is_first:
                            o_T(g, 3)
                    if not is_last:
                        if u == 2:
                            prep_c(g)
                        if u == 3:
                            prep_x(g)
                        if u in (7, 8, 12):
                            project_v(g, (7, 8, 12).index(u))
                    if not is_first:
                        if u == 2:
                            a_T(g, 3)
                        if u == 3:
                            y_out(g, 3)
                        if u == 9:
                            x2_T(g, 1 - par)
                        if u == 10:
                            logits(g)
                    if u in (5, 9, 13):
                        o_T(g, (u - 5) // 4)
                    if u == 5 and not is_last:
                        prep_q(g)
                    if u == 13 and not is_first:
                        rank(g)
                    if u in (6, 10, 14):
                        a_T(g, (u - 6) // 4)
                    if is_first and u == 7:
                        pe.wait_ge(w_in2, 16 * 5)
                    if u in (7, 11, 15):
                        y_out(g, (u - 7) // 4)

            pe.wait_ge(ident_here, 16)
            prep_c(-1)
            pe.wait_ge(wk_here, 32)
            prep_k(-1)
            prep_x(-1)
            pe.wait_ge(wq_here, 32)
            prep_q(-1)
            pe.wait_ge(w_in, 16 * 4)
            project_v(-1, 0)
            project_v(-1, 1)
            project_v(-1, 2)
            pe.wait_ge(setup, 2)
            scores(0, 0, 0)
            scores(0, 0, 1)
            bodies(pe, body)
            values(NG, -1)
            o_T(NG, 3)
            a_T(NG, 3)
            y_out(NG, 3)
            x2_T(NG, 1)
            logits(NG)
            rank(NG)
            wait(pe, tail_free, 12 * NG)
            pe.wait_ge(route_c, ROUTE * NG)
            nc.tensor.matmul(tail[:, 0:E], ones[:, :], mcarry[:, :], start=True, stop=True).then_inc(cnt_full, 1)
            pe.wait_ge(table_c, TABLE)
            pe.wait_ge(ffn_in, 16 * 2)

            def x_T(i, r, turn):
                pe.wait_ge(x_tile[r], 16 * (turn + 1))
                if not (isinstance(i, int) and i == 1):
                    wait(pe, xl_done, i)
                for h in range(2):
                    last = nc.tensor.transpose(x_bank(i)[:, h * P:(h + 1) * P], xt[:, r, h, 0:D], ident[:, :])
                last.then_inc(xT_full, 1)

            def up(i, r, e):
                pe.wait_ge(xl_done, i + 1)
                wait(pe, h_done, MC * (i - 2))
                for c in range(MC):
                    o = h_bank[r][c // 2][:, (c % 2) * TR:(c % 2) * TR + TR]
                    cols = slice(c * P, (c + 1) * P)
                    nc.tensor.matmul(o, w1_hi[:, e, cols], xh[:, r, :], start=True, stop=False)
                    nc.tensor.matmul(o, w1_hi[:, e, cols], xl[:, r, :], start=False, stop=False)
                    nc.tensor.matmul(o, w1_lo[:, e, cols], xh[:, r, :], start=False, stop=True).then_inc(h_full, 1)

            def down(i, r, e):
                wait(pe, yb_done, i)
                pe.wait_ge(hlo_done, i + 1)
                for h in range(2):
                    for c in range(MC):
                        o, rows, cols = y_bank[:, h * D:(h + 1) * D], slice(c * TR + h * P, c * TR + (h + 1) * P), slice(c * D, (c + 1) * D)
                        nc.tensor.matmul(o, h_hi[:, r, rows], w2_hi[:, e, cols], start=(c == 0), stop=False, skip_group_check=True)
                        nc.tensor.matmul(o, h_hi[:, r, rows], w2_lo[:, e, cols], start=False, stop=False, skip_group_check=True)
                        last = nc.tensor.matmul(o, h_lo[:, r, rows], w2_hi[:, e, cols], start=False, stop=(c == MC - 1), skip_group_check=True)
                last.then_inc(y_full, 1)

            e = experts(pe, 0)
            x_T(0, 0, 0)
            x_T(1, 1, 0)
            up(0, 0, e[0])
            x_T(2, 2, 0)
            up(1, 1, e[1])

            def tiles(n, is_last):
                e = experts(pe, n)
                for r in range(PING if is_last else TURN):
                    i = n * TURN + r
                    if not is_last:
                        x_T(i + 3, r % PING, n * 2 + r // PING + 1)
                    if not is_last or r < PING - 2:
                        up(i + 2, (r + 2) % PING, e[r + 2])
                    down(i, r % PING, e[r])

            tiles(0, False)
            with pe.Fori(1, TURNS) as n:
                tiles(n, False)
            tiles(TURNS, True)

        @block.scalar
        def _(act):
            def col(t, i):
                return t[:, i:i + 1] if isinstance(i, int) else t[:, bass.ds(i, 1)]

            copy = lambda out_, in_: nc.scalar.activation(out_, in_, ACT.Copy)

            def exp(g, u):
                act.wait_ge(scoredT, UPG * g + u + 1)
                wait(act, pv_done, UPG * g + u - 3)
                nc.scalar.activation(probs[:, u % 4].rearrange("p j q -> p (j q)"), t_bank[u % 2][:, :], ACT.Exp,
                                     scale=DK ** -0.5).then_inc(exped, 1)

            def prep_copy(g, what, dst):
                act.wait_ge(prep_full, prep_use(g, what) + 1)
                copy(dst, bank_of(g, what)[:, :]).then_inc(xc_done, 1)

            def split_hi(g, t, n):
                act.wait_ge(prep_full, prep_use(g, t.upper()) + 1)
                wait(act, bounced[t], 16 * 4 * (g + 1))
                nc.scalar.activation(parts[t][:, 0, :], bank_of(g, t.upper())[:, :], ACT.Identity, bias=(bq_c if t == "q" else bk_c)[:, 0:1]).then_inc(hi_done, 1)

            def ln1(g, batches):
                act.wait_ge(ln1_rs, RSTEPS * (g + 2 if isinstance(g, int) and g < 1 else NG // 2 + 1))
                for b in batches:
                    last = nc.scalar.activation(xn[:, b, :], x_all[:, g * GB + GB + b, :], ACT.Identity, bias=col(nb1, g * GB + GB + b), scale=col(rs1, g * GB + GB + b))
                if b == GB - 1:
                    last.then_inc(ln1_done, 1)

            def o_copy(g, b):
                done = NS * (GB * g + (b + 1 if b < 3 else 0))
                act.wait_ge(pv_done, done)
                if b < 3 and isinstance(g, int) and g == 0 and b == 0:
                    pass
                else:
                    act.wait_ge(tail_full, (tail_use(g - 1, "OT2") if b == 3 else tail_use(g, "OT3" if b == 0 else f"OT{b - 1}")) + 1)
                copy(o_sb[:, :], o_bank[b % 2][:, :]).then_inc(o_out, 1)

            def a_copy(g, b):
                act.wait_ge(tail_full, tail_use(g, f"aT{b}") + 1)
                copy(aT[:, :], tail[:, 0:P]).then_inc(tail_free, 1)

            def ln2(g, par, pairs, batches, last_one=0):
                act.wait_ge(ln2_rs, RSTEPS * (g + last_one))
                act.wait_ge(scattered[par], GB * TOPK * 16 * pairs + 16)
                for b in batches:
                    last = nc.scalar.activation(pay[:, par, b, :, 0:D], x_all[:, g * GB - GB + b, :].unsqueeze(1).broadcast_to([P, TOPK, D]), ACT.Identity,
                                                bias=nb2[:, b:b + 1], scale=rs2[:, b:b + 1])
                if b == GB - 1:
                    last.then_inc(ln2_done, 1)

            def x2_copy(g):
                act.wait_ge(prep_full, prep_use(g, "x2T") + 1)
                copy(x2T[:, :], prep[:, :]).then_inc(x2T_done, 1)

            def w1_split(g):
                act.wait_ge(w1_ready, 16 * (g + 1))
                nc.scalar.activation(w1_hi[:, g, :], w1_stage[:, :], ACT.Copy, scale=W_SCALE).then_inc(w1hi_done, 1)

            def w2_split(g):
                act.wait_ge(w2_ready, 16 * (g + 1))
                nc.scalar.activation(w2_hi[:, g, :], w2_stage[:, :], ACT.Copy, scale=W_SCALE).then_inc(w2hi_done, 1)

            def body(g, par, is_first, is_last, pairs):
                for u in range(UPG):
                    exp(g, u)
                    if not is_last:
                        if u == 2:
                            prep_copy(g, "cT", cT[:, :])
                        if u < 3:
                            ln1(g, ((0,), (1, 2), (3,))[u])
                        if u == 3:
                            prep_copy(g, "xT", xnT[:, :])
                        if u in (4, 5):
                            split_hi(g, "kq"[u - 4], u - 4)
                    if not is_first:
                        if u == 0:
                            o_copy(g, 3)
                        if u == 2:
                            a_copy(g, 3)
                        if u in (6, 7, 8):
                            ln2(g, 1 - par, pairs, ((0,), (1, 2), (3,))[u - 6])
                        if u == 9:
                            x2_copy(g)
                    if u in (4, 8, 12):
                        o_copy(g, u // 4 - 1)
                    if u in (6, 10, 14):
                        a_copy(g, (u - 6) // 4)
                    if u == 13:
                        w1_split(g)
                    if u == 15:
                        w2_split(g)

            prep_copy(-1, "cT", cT[:, :])
            act.wait_ge(wk_here, 32)
            split_hi(-1, "k", 0)
            prep_copy(-1, "xT", xnT[:, :])
            act.wait_ge(wq_here, 32)
            split_hi(-1, "q", 1)
            act.wait_ge(w_in, 16 * 4)
            nc.scalar.activation(gate[:, :], gate_in[:, :], ACT.Tanh).then_inc(gates_done, 1)
            bodies(act, body)
            o_copy(NG, 3)
            a_copy(NG, 3)
            ln2(NG, 1, NG // 2 - 1, range(GB - 1))
            ln2(NG, 1, NG // 2 - 1, (GB - 1,), 1)
            x2_copy(NG)
            act.wait_ge(table_c, T_FILL)
            for e in range(1, E, 2):
                at = act.value_load(fill_i[0:1, e:e + 1], min_val=e * RS, max_val=e * RS + NTOK)
                act.dma_start(rows_dram[bass.ds(at, TR), :].rearrange("(p h) c -> p h c", h=2), pad[:, :, :]).then_inc(filled, 16)
            act.wait_ge(dz_done, 1)
            nc.scalar.activation(ez[:, :, :], dz[:, :, :], ACT.Exp).then_inc(ez_done, 1)
            nc.scalar.activation(gelu_warm[:, :], gate[:, 0:1], ACT.Gelu).then_inc(warm, 1)
            act.wait_ge(table_c, TABLE)
            act.wait_ge(ffn_in, 16 * 2)

            def x_hi(i, r):
                act.wait_ge(xT_full, i + 1)
                copy(xh[:, r, :], x_bank(i)[:, 0:TR]).then_inc(xh_done, 1)

            def gelu(i, r, e):
                wait(act, hlo_done, i - PING + 1)
                for c in range(MC):
                    act.wait_ge(h_full, MC * i + c + 1 if c % 2 else MC * i + c + 2)
                    nc.scalar.activation(hT[:, r, c * TR:(c + 1) * TR], h_bank[r][c // 2][:, (c % 2) * TR:(c % 2) * TR + TR], ACT.Gelu,
                                         bias=b1_c[:, e, c:c + 1], scale=1.0 / W_SCALE).then_inc(h_done, 1)

            def h_high(i, r):
                act.wait_ge(h_done, MC * i + MC)
                wait(act, y_full, i - PING + 1)
                copy(h_hi[:, r, :], hT[:, r, :]).then_inc(hhi_done, 1)

            e = experts(act, 0)
            x_hi(0, 0)
            x_hi(1, 1)
            gelu(0, 0, e[0])
            x_hi(2, 2)
            h_high(0, 0)

            def tiles(n, is_last):
                e = experts(act, n)
                for r in range(PING if is_last else TURN):
                    i = n * TURN + r
                    if not is_last or r < PING - 1:
                        gelu(i + 1, (r + 1) % PING, e[r + 1])
                    if not is_last:
                        x_hi(i + 3, r % PING)
                    if not is_last or r < PING - 1:
                        h_high(i + 1, (r + 1) % PING)

            tiles(0, False)
            with act.Fori(1, TURNS) as n:
                tiles(n, False)
            tiles(TURNS, True)

            act.wait_ge(weight_c, WSTEPS)
            for g in range(NG):
                act.wait_ge(y_ready[g], 16 * TOPK)
                for b in range(GB):
                    last = nc.scalar.activation(y_in[:, g, 1, b, :], y_in[:, g, 1, b, :], ACT.Copy, scale=weight[:, g * GB + b, 1:2])
                last.then_inc(weighted, 1)

        @block.vector
        def _(dve):
            vec = nc.vector

            def maxima(g, u):
                dve.wait_ge(scored, UPG * g + u + 1)
                vec.reduce_max(maxes[:, u, :], s_bank[u % 2][:, :].rearrange("p (j k) -> p j k", j=NJ), AX_X).then_inc(maxed, 1)

            def v_out(g, b):
                dve.wait_ge(prep_full, prep_use(g, f"V{b}") + 1)
                vec.tensor_tensor(v_aug[:, b, :, 0:DK], bank_of(g, f"V{b}")[:, 0:D].rearrange("p (h d) -> p h d", h=NH),
                                  bv_b[:, :].rearrange("p (h d) -> p h d", h=NH), ALU.add).then_inc(v_done, 1)

            def split_lo(g, t, n):
                dve.wait_ge(hi_done, 2 * g + 2 + n + 1)
                wait(dve, bounced[t], 16 * 4 * (g + 1))
                vec.scalar_tensor_tensor(parts[t][:, 1, :], bank_of(g, t.upper())[:, :], (bq_c if t == "q" else bk_c)[:, 0:1], parts[t][:, 0, :],
                                         ALU.add, ALU.subtract).then_inc(lo_done, 1)

            def normalise(g, b):
                at = (GB * g + b) if b < 3 else GB * g - 1
                dve.wait_ge(tail_full, tail_use(g, f"OT{b}") + 1)
                heads = tail[:, :].rearrange("p (s j w) -> p s j w", s=NS, j=NJ)
                vec.reciprocal(rl[:, :, :], heads[:, :, :, DK]).then_inc(norm_c, 1)
                dve.wait_ge(norm_c, at + 1)
                vec.tensor_tensor(a_sb[:, :].rearrange("p (j s d) -> p s j d", j=NJ, s=NS), heads[:, :, :, 0:DK],
                                  rl[:, :, :].unsqueeze(3).broadcast_to([P, NS, NJ, DK]), ALU.mult).then_inc(tail_free, 1)

            def residual(g, b):
                at = (GB * g + b) if b < 3 else GB * g - 1
                if b == 0:
                    dve.wait_ge(x_plus, g + 1)
                dve.wait_ge(tail_full, tail_use(g, f"y{b}") + 1)
                vec.scalar_tensor_tensor(x_all[:, at, :], tail[:, 0:D], gate[:, 0:1], x_all[:, at, :], ALU.mult, ALU.add).then_inc(tail_free, 1)

            def stats2(g, b):
                at = (GB * g + b) if b < 3 else GB * g - 1
                dve.wait_ge(tail_free, tail_use(g, f"y{b}") + 1)
                apart(dve)
                vec.bn_stats(st2[:, b, :], x_all[:, at, :]).then_inc(ln2_stats, 1)

            def aggregate2(g, b, par):
                at = (GB * g + b) if b < 3 else GB * g - 1
                dve.wait_ge(ln2_stats, 2 * at + 1)
                apart(dve)
                vec.bn_aggr(mv2[:, par, b, :], st2[:, b, :]).then_inc(ln2_stats, 1)

            def stats1(group):
                for b in range(group * GB, group * GB + GB):
                    last = vec.bn_stats(st1[:, b, :], x_all[:, b, :])
                last.then_inc(ln1_stats, 1)

            def aggregate1(group):
                dve.wait_ge(ln1_stats, group + 1)
                for b in range(group * GB, group * GB + GB):
                    last = vec.bn_aggr(mv1[:, b, :], st1[:, b, :])
                last.then_inc(ln1_mean, 1)

            def after(g, step):
                dve.wait_ge(route_c, ROUTE * (g - 1) + step)

            def route_logits(g):
                dve.wait_ge(prep_full, prep_use(g, "logits") + 1)
                vec.tensor_tensor(lg[:, :, :], prep[:, 0:GB * E].rearrange("p (b e) -> p b e", b=GB),
                                  br_b[:, :].unsqueeze(1).broadcast_to([P, GB, E]), ALU.add).then_inc(lg_done, 1)

            def route_max(g):
                dve.wait_ge(lg_done, 2 * g + 1)
                apart(dve)
                for b in range(GB):
                    last = vec.max(t8[:, b, :], lg[:, b, :])
                last.then_inc(route_c, 1)

            def route_index(g):
                after(g, R_MAX)
                apart(dve)
                for b in range(GB):
                    last = vec.max_index(ti[:, b, :], t8[:, b, :], lg[:, b, :])
                last.then_inc(route_c, 1)
                vec.tensor_copy(t8_all[:, bass.ds((g - 1) * GB, GB), :], t8[:, :, :]).then_inc(kept, 1)

            def route_masks(g):
                after(g, R_INDEX)
                for k in range(TOPK):
                    last = vec.tensor_tensor(mk[:, :, k, :], consts[:, C_IOTA:C_IOTA + E].unsqueeze(1).broadcast_to([P, GB, E]),
                                             ti[:, :, k:k + 1].broadcast_to([P, GB, E]), ALU.is_equal)
                last.then_inc(route_c, 1)

            def route_both(g):
                after(g, R_MASK)
                vec.tensor_tensor(mboth[:, :, :], mk[:, :, 0, :], mk[:, :, 1, :], ALU.add).then_inc(route_c, 1)

            def route_sum(g):
                after(g, R_BOTH)
                vec.reduce_sum(msum[:, :], mboth[:, :, :].rearrange("p b e -> p e b"), AX_X).then_inc(route_c, 1)

            def route_rank(g):
                dve.wait_ge(prep_full, prep_use(g, "rank") + 1)
                vec.tensor_tensor(rank_b[:, :, :], prep[:, 0:GB * E].rearrange("p (b e) -> p b e", b=GB),
                                  consts[:, C_BASE:C_BASE + E].unsqueeze(1).broadcast_to([P, GB, E]), ALU.add).then_inc(lg_done, 1)

            def route_select(g):
                dve.wait_ge(lg_done, 2 * g + 2)
                after(g, R_SUM)
                for k in range(TOPK):
                    last = vec.tensor_tensor(sel[:, :, k, :], mk[:, :, k, :], rank_b[:, :, :], ALU.mult)
                last.then_inc(route_c, 1)

            def route_slot(g):
                after(g, R_SEL)
                vec.reduce_sum(slot_f[:, :, :], sel[:, :, :, :], AX_X).then_inc(route_c, 1)

            def route_slot_i(g, par):
                after(g, R_SLOT)
                vec.tensor_copy(slot_i[:, par, :], slot_f[:, :, :].rearrange("p b k -> p (b k)")).then_inc(route_c, 1)
                vec.tensor_tensor(mcarry[:, :], mcarry[:, :], msum[:, :], ALU.add).then_inc(route_c, 1)

            def w1_low(g):
                dve.wait_ge(w1hi_done, g + 1)
                vec.scalar_tensor_tensor(w1_lo[:, g, :], w1_stage[:, :], W_SCALE, w1_hi[:, g, :], ALU.mult, ALU.subtract).then_inc(w1lo_done, 1)

            def w2_low(g):
                dve.wait_ge(w2hi_done, g + 1)
                vec.scalar_tensor_tensor(w2_lo[:, g, :], w2_stage[:, :], W_SCALE, w2_hi[:, g, :], ALU.mult, ALU.subtract).then_inc(w2lo_done, 1)

            def body(g, par, is_first, is_last, pairs):
                for u in range(UPG):
                    if u < UPG - 2:
                        maxima(g, u + 2)
                    elif not is_last:
                        maxima(g + 1, u + 2 - UPG)
                    if u == 1:
                        v_out(g, 3)
                    if u == 4 and not is_first:
                        aggregate2(g, 3, 1 - par)
                    if not is_last:
                        if u == 4:
                            split_lo(g, "k", 0)
                        if u in (7, 8, 12):
                            v_out(g, (7, 8, 12).index(u))
                    if is_first:
                        if u == 4:
                            dve.wait_ge(x_rest, 16)
                        if u in (4, 6, 8, 10, 11, 12):
                            stats1((4, 6, 8, 10, 11, 12).index(u) + 2)
                        if u in (5, 7, 9, 11, 12, 13):
                            aggregate1((5, 7, 9, 11, 12, 13).index(u) + 2)
                    if not is_first:
                        if u == 1:
                            normalise(g, 3)
                        if u == 3:
                            residual(g, 3)
                            stats2(g, 3)
                        if u == 10:
                            route_logits(g)
                        if u == 11:
                            route_max(g)
                    if u in (5, 9, 13):
                        normalise(g, (u - 5) // 4)
                    if u == 5 and not is_last:
                        split_lo(g, "q", 1)
                    if u in (7, 11, 15):
                        residual(g, (u - 7) // 4)
                    if not is_first:
                        if u == 11:
                            route_index(g)
                        if u == 12:
                            route_masks(g)
                    if u == 0 and not is_first:
                        w1_low(g - 1)
                    if u == 2 and not is_first:
                        w2_low(g - 1)
                    if not is_first:
                        if u == 12:
                            route_both(g)
                            route_sum(g)
                        if u == 13:
                            route_rank(g)
                        if u == 14:
                            route_select(g)
                            route_slot(g)
                            route_slot_i(g, 1 - par)
                    if u in (8, 12):
                        stats2(g, (u - 8) // 4)
                    if u in (9, 13):
                        aggregate2(g, (u - 9) // 4, par)
                stats2(g, 2)
                aggregate2(g, 2, par)

            vec.memset(diag["k"][:, 0].rearrange("p j s t -> p (j s t)").bitcast(U32), 0).then_inc(zeroed["k"][0], 1)
            dve.wait_ge(x_first, 16)
            stats1(0)
            aggregate1(0)
            vec.memset(ones[:, :], 1.0)
            vec.memset(mcarry[:, :], 0.0)
            vec.memset(ones8[:, :], 1.0).then_inc(setup, 1)
            dve.sem_inc(lg_done, 2)
            dve.wait_ge(ident_here, 16)
            vec.tensor_scalar(neg_ident[:, :], ident[:, :], -1.0, None, ALU.mult).then_inc(setup, 1)
            dve.wait_ge(ln1_rs, RSTEPS)
            for b in range(GB):
                last = vec.tensor_scalar(xn[:, b, :], x_all[:, b, :], rs1[:, b:b + 1], nb1[:, b:b + 1], ALU.mult, ALU.add)
            last.then_inc(ln1_done, 1)
            dve.wait_ge(wk_here, 32)
            split_lo(-1, "k", 0)
            dve.wait_ge(wq_here, 32)
            split_lo(-1, "q", 1)
            dve.wait_ge(w_in, 16 * 4)
            dve.wait_ge(v_zeroed, 2)
            for b in range(GB - 1):
                v_out(-1, b)
            dve.wait_ge(gates_done, 1)
            vec.tensor_scalar(gbo[:, :], bo_b[:, :], gate[:, 0:1], None, ALU.mult).then_inc(gbo_done, 1)
            dve.wait_ge(x_second, 16)
            stats1(1)
            aggregate1(1)
            dve.wait_ge(w_in2, 16 * 5)
            vec.tensor_copy(tri[:, :], tri32[:, :]).then_inc(setup, 1)
            maxima(0, 0)
            maxima(0, 1)
            bodies(dve, body)
            w1_low(NG - 1)
            w2_low(NG - 1)
            normalise(NG, 3)
            residual(NG, 3)
            stats2(NG, 3)
            aggregate2(NG, 3, 1)
            for piece in (route_logits, route_max, route_index, route_masks, route_both, route_sum, route_rank, route_select, route_slot):
                piece(NG)
            route_slot_i(NG, 1)

            c = Chain(dve, table_c, TABLE, 0)
            dve.wait_ge(cnt_full, 1)
            c.link(vec.tensor_copy(cnt[:, :], tail[:, 0:E]))
            c.link(vec.tensor_tensor(fill_f[:, :], cnt[:, :], consts[:, C_BASE:C_BASE + E], ALU.add))
            c.step(vec.tensor_copy(fill_i[:, :], fill_f[:, :]))
            c.link(vec.tensor_tensor(over[:, :, :], cnt[:, :].unsqueeze(2).broadcast_to([P, E, MAXT]),
                                     consts[:, C_STEP:C_STEP + MAXT].unsqueeze(1).broadcast_to([P, E, MAXT]), ALU.is_gt))
            c.link(vec.reduce_sum(ntile[:, :], over[:, :, :], AX_X))
            c.link(vec.tensor_tensor_scan(ntile_end[:, :], ones8[:, :], ntile[:, :], 0.0, ALU.mult, ALU.add))
            tiles_c = consts[:, C_TILE:C_TILE + (TURNS + 1) * AHEAD]
            turns = lambda t: t.rearrange("p (n k) -> p n k", k=AHEAD)
            c.link(vec.tensor_tensor(past[:, :, :], tiles_c.unsqueeze(2).broadcast_to([P, (TURNS + 1) * AHEAD, E]),
                                     ntile_end[:, :].unsqueeze(1).broadcast_to([P, (TURNS + 1) * AHEAD, E]), ALU.is_ge))
            c.step(vec.reduce_sum(te[:, :], past[:, :, :], AX_X))
            c.link(vec.tensor_tensor(pastn[:, :, :], past[:, :, :], ntile[:, :].unsqueeze(1).broadcast_to([P, (TURNS + 1) * AHEAD, E]), ALU.mult))
            c.link(vec.reduce_sum(tprev[:, :], pastn[:, :, :], AX_X))
            c.link(vec.tensor_tensor(ta[:, :], tiles_c, tprev[:, :], ALU.subtract))
            c.link(vec.tensor_scalar(tb[:, :], te[:, :], float(RS), None, ALU.mult))
            c.link(vec.scalar_tensor_tensor(tr[:, :], ta[:, :], float(TR), tb[:, :], ALU.mult, ALU.add))
            c.step(vec.tensor_scalar(tile_row[:, :, 0:AHEAD], turns(tr[:, :]), float(E * RS), None, ALU.min))
            c.link(vec.tensor_scalar(digits[:, :, :], turns(te[:, :]), float(E - 1), None, ALU.min))
            c.link(vec.tensor_tensor(digits[:, :, :], digits[:, :, :], consts[:, C_DIGIT:C_END].unsqueeze(1).broadcast_to([P, TURNS + 1, AHEAD]), ALU.mult))
            c.link(vec.reduce_sum(packed_f[:, :], digits[:, :, :], AX_X))
            c.link(vec.tensor_copy(packed[:, :], packed_f[:, :]))

            dve.wait_ge(kept, NG)
            vec.tensor_tensor(dz[:, :, :], t8_all[:, :, :], t8_all[:, :, 0:1].broadcast_to([P, NB, E]), ALU.subtract).then_inc(dz_done, 1)
            dve.wait_ge(ez_done, 1)
            c = Chain(dve, weight_c, WSTEPS, 0)
            c.link(vec.reduce_sum(z1[:, :], ez[:, :, :], AX_X))
            c.link(vec.reciprocal(z2[:, :], z1[:, :]))
            c.link(vec.tensor_tensor(pk[:, :, :], ez[:, :, 0:TOPK], z2[:, :].unsqueeze(2).broadcast_to([P, NB, TOPK]), ALU.mult))
            c.link(vec.reduce_sum(z3[:, :], pk[:, :, :], AX_X))
            c.link(vec.tensor_scalar(z4[:, :], z3[:, :], MOE_EPS, None, ALU.add))
            c.link(vec.reciprocal(z5[:, :], z4[:, :]))
            c.link(vec.tensor_tensor(wk2[:, :, :], pk[:, :, :], z5[:, :].unsqueeze(2).broadcast_to([P, NB, TOPK]), ALU.mult))
            c.link(vec.reduce_sum(z6[:, :], wk2[:, :, :], AX_X))
            c.link(vec.tensor_scalar(z7[:, :], z6[:, :], MOE_EPS, None, ALU.add))
            c.link(vec.reciprocal(z8[:, :], z7[:, :]))
            c.step(vec.scalar_tensor_tensor(weight[:, :, :], wk2[:, :, :], gate[:, 1:2], z8[:, :].unsqueeze(2).broadcast_to([P, NB, TOPK]),
                                            ALU.mult, ALU.mult))

            dve.wait_ge(ffn_in, 16 * 2)

            def x_lo(i, r):
                dve.wait_ge(xh_done, i + 1)
                vec.tensor_tensor(xl[:, r, :], x_bank(i)[:, 0:TR], xh[:, r, :], ALU.subtract).then_inc(xl_done, 1)

            def keep_rows(i, r):
                dve.wait_ge(xT_full, i + 1)
                wait(dve, dest_done, i - PING + 1)
                vec.tensor_copy(row_ids[:, r, :], xt[:, r, :, D]).then_inc(taken, 1)

            def y_end(i, r, turn, e):
                dve.wait_ge(y_full, i + 1)
                wait(dve, y_tile[r], 32 * turn)
                vec.scalar_tensor_tensor(yb[:, r], y_bank[:, 0:2 * D].rearrange("p (h d) -> p h d", h=2), 1.0 / W_SCALE,
                                         b2_b[:, e, :].unsqueeze(1).broadcast_to([P, 2, D]), ALU.mult, ALU.add).then_inc(yb_done, 1)
                dve.wait_ge(taken, i + 1)
                vec.tensor_copy(dest[:, r, :], row_ids[:, r, :]).then_inc(dest_done, 1)

            def h_low(i, r):
                dve.wait_ge(hhi_done, i + 1)
                wait(dve, y_full, i - PING + 1)
                vec.tensor_tensor(h_lo[:, r, :], hT[:, r, :], h_hi[:, r, :], ALU.subtract).then_inc(hlo_done, 1)

            for r in range(PING):
                x_lo(r, r)
                if r < PING - 1:
                    keep_rows(r, r)
            h_low(0, 0)

            def tiles(n, is_last):
                size = PING if is_last else TURN
                e = experts(dve, n)
                for r in range(size):
                    i = n * TURN + r
                    if not is_last:
                        x_lo(i + 3, r % PING)
                    if not is_last or r < PING - 2:
                        keep_rows(i + 2, (r + 2) % PING)
                    if not is_last or r < PING - 1:
                        h_low(i + 1, (r + 1) % PING)
                    y_end(i, r % PING, n * 2 + r // PING, e[r])

            tiles(0, False)
            with dve.Fori(1, TURNS) as n:
                tiles(n, False)
            tiles(TURNS, True)

            dve.wait_ge(weight_c, WSTEPS)

            def add_first(g):
                dve.wait_ge(y_ready[g], 16 * TOPK)
                for b in range(GB):
                    at = g * GB + b
                    last = vec.scalar_tensor_tensor(x_all[:, at, :], y_in[:, g, 0, b, :], weight[:, at, 0:1], x_all[:, at, :], ALU.mult, ALU.add)
                last.then_inc(first_added, 1)

            add_first(0)
            for g in range(NG):
                if g < NG - 1:
                    add_first(g + 1)
                dve.wait_ge(first_added, g + 1)
                dve.wait_ge(weighted, g + 1)
                rows = x_all[:, g * GB:(g + 1) * GB, :]
                vec.tensor_tensor(rows, rows, y_in[:, g, 1], ALU.add).then_inc(summed, 1)

        @block.gpsimd
        def _(pool):
            gp = nc.gpsimd

            def rstd(sem_, n, rs, nb, mv, k):
                c = Chain(pool, sem_, RSTEPS, n)
                apart(pool)
                c.link(gp.tensor_scalar(rs, mv[:, :, 1], LN_EPS, 1.0, ALU.add, ALU.mult))
                c.link(gp.tensor_tensor(rs, rs, neg_half[:, 0:k], ALU.pow))
                apart(pool)
                c.link(gp.tensor_scalar(nb, mv[:, :, 0], -1.0, 0.0, ALU.mult, ALU.add))
                c.step(gp.tensor_tensor(nb, nb, rs, ALU.mult))

            def rstd1(n, first, end):
                pool.wait_ge(ln1_mean, end)
                b = slice(first * GB, end * GB)
                rstd(ln1_rs, n, rs1[:, b], nb1[:, b], mv1[:, b], (end - first) * GB)

            def rstd2(g, par):
                pool.wait_ge(ln2_stats, 2 * GB * g)
                rstd(ln2_rs, g - 1, rs2[:, :], nb2[:, :], mv2[:, par], GB)

            def rstd2_of(n, b):
                pool.wait_ge(ln2_stats, 2 * (GB * (NG - 1) + b.stop))
                rstd(ln2_rs, n - 1, rs2[:, b], nb2[:, b], mv2[:, 1, b], b.stop - b.start)

            def add_bias(g):
                pool.wait_ge(ln1_done, g + 2)
                apart(pool)
                x4 = x_all[:, bass.ds(g * GB + GB, GB), :]
                gp.tensor_tensor(x4, x4, gbo[:, :].unsqueeze(1).broadcast_to([P, GB, D]), ALU.add).then_inc(x_plus, 1)

            def scatter(g, par, batches=range(GB)):
                if batches[0] == 0:
                    fill_ids(g, par)
                for b in batches:
                    for k in range(TOPK):
                        gp.indirect_dma_start(out=rows_dram, out_offset=bass.IndirectOffsetOnAxis(ap=slot_i[:, par, b * TOPK + k:b * TOPK + k + 1], axis=0),
                                              in_=pay[:, par, b, k, :], in_offset=None).then_inc(scattered[par], 16)

            def fill_ids(g, par):
                pool.wait_ge(ln2_done, g)
                apart(pool)
                ids = consts[:, bass.ds((g - 1) * (GB * TOPK) + C_ID, GB * TOPK)]
                gp.tensor_copy(pay[:, par, :, :, D],
                               ids.rearrange("p (b k) -> p b k", b=GB)).then_inc(ids_done, 1)
                pool.wait_ge(ids_done, g)
                pool.wait_ge(route_c, ROUTE * g)
                apart(pool)

            def body(g, par, is_first, is_last, pairs):
                if not is_first:
                    rstd2(g, 1 - par)
                if not is_last:
                    add_bias(g)
                if is_first:
                    for n in range(1, NG // 2):
                        rstd1(n + 1, 2 * n, 2 * n + 2)
                if not is_first:
                    scatter(g, 1 - par, range(GB // 2 - 1 if is_last else GB))

            def zero(t, par):
                gp.memset(diag[t][:, par].rearrange("p j s t -> p (j s t)").bitcast(U32), 0).then_inc(zeroed[t][par], 1)

            gp.memset(neg_half[:, :], -0.5).then_inc(half_done, 1)
            pool.wait_ge(half_done, 1)
            rstd1(0, 0, 1)
            zero("q", 0)
            gp.memset(v_aug[:, :, :, :], 0.0).then_inc(v_zeroed, 1)
            pool.wait_ge(v_zeroed, 1)
            gp.memset(v_aug[:, :, :, DK], 1.0).then_inc(v_zeroed, 1)
            rstd1(1, 1, 2)
            for t in "kq":
                zero(t, 1)
            pool.wait_ge(gbo_done, 1)
            add_bias(-1)
            gp.memset(pad[:, :, :], 0.0).then_inc(pad_done, 1)
            pool.wait_ge(pad_done, 1)
            gp.memset(pad[:, :, D], NOWHERE).then_inc(pad_done, 1)
            pool.wait_ge(pad_done, 2)
            for i in range(2):
                gp.dma_start(rows_dram[E * RS + i * P:E * RS + (i + 1) * P, :], pad[:, i, :]).then_inc(scattered[i], 16)
            bodies(pool, body)
            rstd2_of(NG, slice(0, GB - 1))
            scatter(NG - 1, 0, (GB // 2 - 1,))
            rstd2_of(NG + 1, slice(GB - 1, GB))
            scatter(NG - 1, 0, range(GB // 2, GB))
            scatter(NG, 1)

            def put(i, r):
                pool.wait_ge(yb_done, i + 1)
                pool.wait_ge(dest_done, i + 1)
                apart(pool)
                for h in range(2):
                    gp.indirect_dma_start(out=y_dram, out_offset=bass.IndirectOffsetOnAxis(ap=dest[:, r, h:h + 1], axis=0), in_=yb[:, r, h, :],
                                          in_offset=None, bounds_check=TOPK * NTOK - 1, oob_is_err=False).then_inc(y_tile[r], 16)

            with pool.Fori(0, NT // PING) as n:
                for r in range(PING):
                    put(n * PING + r, r)


_INS = ['x', 'ctx_in', 'gates', 'wq', 'bq', 'wk', 'bk', 'wv', 'bv', 'wo', 'bo', 'wr', 'br', 'w1', 'b1', 'w2', 'b2', 'ident', 'tri', 'consts']


def kernel(**inputs):
    import concourse.bacc as _bacc
    from concourse.bass_utils import run_bass_kernel_spmd as _run

    a = {k: np.asarray(v) for k, v in inputs.items()}

    def by_block(w):
        return w.reshape(w.shape[:-1] + (NJ, NS, DK)).swapaxes(-1, -2).reshape(w.shape)

    consts = np.zeros(C_END, np.float32)
    consts[C_IOTA:C_IOTA + E] = np.arange(E)
    consts[C_BASE:C_BASE + E] = np.arange(E) * RS
    consts[C_TILE:C_TILE + (TURNS + 1) * AHEAD] = np.minimum(np.arange(TURNS + 1)[:, None] * TURN + np.arange(AHEAD), NT - 1).reshape(-1)
    consts[C_STEP:C_STEP + MAXT] = np.arange(MAXT) * TR
    consts = np.tile(consts, (P, 1))
    consts[:, C_DIGIT:C_END] = float(E) ** np.arange(AHEAD)
    token = np.arange(NB)[None, :, None] * P + np.arange(P)[:, None, None]
    consts[:, C_ID:C_DIGIT] = (token + np.arange(TOPK)[None, None, :] * NTOK).reshape(P, NB * TOPK)
    host = {
        'x': a['x'], 'ctx_in': a['ctx_1024'], 'gates': np.concatenate([a['g_xattn'], a['g_ffn']]),
        'wq': by_block(a['L0_xattn_W_q'].T), 'bq': by_block(a['L0_xattn_b_q'])[:, None],
        'wk': by_block(a['L0_xattn_W_k'].T), 'bk': by_block(a['L0_xattn_b_k'])[:, None],
        'wv': a['L0_xattn_W_v'].T, 'bv': a['L0_xattn_b_v'], 'wo': a['L0_xattn_W_o'].T, 'bo': a['L0_xattn_b_o'],
        'wr': a['L0_ffn_Wr'], 'br': a['L0_ffn_br'], 'w1': a['L0_ffn_W1'],
        'b1': a['L0_ffn_b1'].reshape(E * MC, P).T,
        'w2': a['L0_ffn_W2'].reshape(E, MC, P, D).transpose(0, 2, 1, 3).reshape(E, P, MC * D), 'b2': a['L0_ffn_b2'],
        'ident': np.eye(P, dtype=np.float32), 'tri': np.triu(np.ones((P, P), np.float32), 1), 'consts': consts,
    }
    nc = _bacc.Bacc("TRN2", target_bir_lowering=False, num_devices=1)
    arrays, args = {}, []
    for name in _INS:
        v = np.ascontiguousarray(host[name])
        arrays["in_" + name] = v
        args.append(nc.dram_tensor("in_" + name, v.shape, mybir.dt.from_np(v.dtype), kind="ExternalInput").ap())
    args.append(nc.dram_tensor("out", (NB, P, D), F32, kind="ExternalOutput").ap())
    moe_attention(nc, *args)
    r = _run(nc, [arrays], core_ids=[0])
    return r.results[0]["out"]
```
